# Optimizing a Trainium2 kernel written in Bass

```python
import numpy as np
import jax
import jax.numpy as jnp

def _softmax(x, axis=-1):
    return jax.nn.softmax(x, axis=axis)

def _gelu(x):
    return jax.nn.gelu(x, approximate=True)

def _silu(x):
    return jax.nn.silu(x)

def _sigmoid(x):
    return jax.nn.sigmoid(x)

def _layernorm(x, axis=-1, eps=1e-05):
    m = jnp.mean(x, axis=axis, keepdims=True)
    v = jnp.var(x, axis=axis, keepdims=True)
    return (x - m) / jnp.sqrt(v + eps)

def _scatter_add(tgt, idx, src, axis=0):
    return tgt.at[idx].add(src)

def _segment_sum(src, seg, n):
    return jax.ops.segment_sum(src, seg, n)
kernel_name = 'mk_flamingo_gated_d1_seqx_r2_beb1ab'

def setup_inputs(seed: int=0):
    np.random.seed(seed)
    _w = jnp.asarray

    def _rec_inputs():
        import jax
        import jax.numpy as jnp
        _rk = jax.random.key(seed)
        x = 0.000341 + 1 * jax.random.normal(jax.random.fold_in(_rk, 1), (8, 512, 1024), jnp.float32)
        _lenS = 512 - jax.random.randint(jax.random.fold_in(_rk, 7), (8,), 0, max(1, 512 // 4) + 1, jnp.int32)
        _lenS2 = 512 - jax.random.randint(jax.random.fold_in(_rk, 8), (8,), 0, max(1, 512 // 4) + 1, jnp.int32)
        _ctx_2048P = jax.random.normal(jax.random.fold_in(_rk, 11), (8, 16, 1024), jnp.float32)
        _ctx_2048c = jax.random.dirichlet(jax.random.fold_in(_rk, 511), 0.3 * jnp.ones((16,), jnp.float32), (8, 512))
        _ctx_2048t = jnp.einsum('bsk,bkd->bsd', _ctx_2048c, _ctx_2048P)
        _ctx_2048t = _ctx_2048t * jax.lax.rsqrt(jnp.mean(jnp.square(_ctx_2048t)) + 1e-12) * 0.953939
        ctx_2048 = -1.47943e-05 + 1.00017 * (_ctx_2048t + 0.3 * jax.random.normal(jax.random.fold_in(_rk, 611), (8, 512, 1024), jnp.float32))
        _g = jax.random.normal(jax.random.fold_in(_rk, 9001), (2, 1), jnp.float32)
        _g = jnp.sign(_g) * jnp.maximum(jnp.abs(_g), 1.0) + (_g == 0) * 1.0
        g_xattn = _g[0]
        g_ffn = _g[1]
        return (x, ctx_2048, g_xattn, g_ffn)
    x, ctx_2048, g_xattn, g_ffn = _rec_inputs()

    def _L0_xattn_setup():
        import jax, jax.numpy as jnp
        import numpy as np

        def _wkv(time_decay, time_first, k, v):
            w = -jnp.exp(time_decay)
            u = time_first
            B, T, C = k.shape
            aa = jnp.zeros((B, C), dtype=k.dtype)
            bb = jnp.zeros((B, C), dtype=k.dtype)
            pp = jnp.full((B, C), -1e+38, dtype=k.dtype)

            def step(carry, kv_t):
                aa, bb, pp = carry
                kt, vt = kv_t
                ww = u + kt
                q = jnp.maximum(pp, ww)
                e1 = jnp.exp(pp - q)
                e2 = jnp.exp(ww - q)
                y_t = (e1 * aa + e2 * vt) / (e1 * bb + e2)
                ww2 = pp + w
                q2 = jnp.maximum(ww2, kt)
                e1b = jnp.exp(ww2 - q2)
                e2b = jnp.exp(kt - q2)
                new_carry = (e1b * aa + e2b * vt, e1b * bb + e2b, q2)
                return (new_carry, y_t)
            ks = jnp.transpose(k, (1, 0, 2))
            vs = jnp.transpose(v, (1, 0, 2))
            _, ys = jax.lax.scan(step, (aa, bb, pp), (ks, vs))
            return jnp.transpose(ys, (1, 0, 2))
        key = jax.random.key(seed)
        k1, k2, k3, k4 = jax.random.split(key, 4)
        B, T, C = (8, 512, 1024)
        return {'batch_size': B, 'seq_len': T, 'embedding_dim': C, 'time_decay': jax.random.normal(k1, (C,), dtype=jnp.float32), 'time_first': jax.random.normal(k2, (C,), dtype=jnp.float32), 'k': jax.random.normal(k3, (B, T, C), dtype=jnp.float32), 'v': jax.random.normal(k4, (B, T, C), dtype=jnp.float32)}
    _L0_xattn_all = _L0_xattn_setup()
    _L0_xattn_in = {k: v for k, v in _L0_xattn_all.items() if k in ('time_decay', 'time_first')}
    del _L0_xattn_all

    def _L0_ffn_setup():
        import jax, jax.numpy as jnp
        import numpy as np
        L, B, D = (1024, 1, 1024)
        H = 16
        DK, DV = (D // 2, D)
        HDK, HDV = (DK // H, DV // H)
        RATIO = 2
        BASE = 10000.0
        EPS = 1e-05

        def _apply_rotary(x, cos, sin):
            d2 = x.shape[-1] // 2
            x1, x2 = (x[..., :d2], x[..., d2:])
            return jnp.concatenate([x1 * cos - x2 * sin, x2 * cos + x1 * sin], axis=-1)
        key = jax.random.key(seed)
        ks = jax.random.split(key, 8)
        s = 0.02
        return {'x': jax.random.normal(ks[0], (L, B, D), jnp.float32), 'conv_w': jax.random.normal(ks[1], (D, 2), jnp.float32) * 0.5, 'Wq': jax.random.normal(ks[2], (D, DK), jnp.float32) * s, 'Wk': jax.random.normal(ks[3], (D, DK), jnp.float32) * s, 'Wv': jax.random.normal(ks[4], (D, DV), jnp.float32) * s, 'Wg': jax.random.normal(ks[5], (D, DV), jnp.float32) * s, 'router_w': jax.random.normal(ks[6], (H, HDV, RATIO), jnp.float32) * s, 'Wout': jax.random.normal(ks[7], (DV, D), jnp.float32) * s}
    _L0_ffn_all = _L0_ffn_setup()
    _L0_ffn_in = {k: v for k, v in _L0_ffn_all.items() if k in ('conv_w', 'Wq', 'Wk', 'Wv', 'Wg', 'router_w', 'Wout')}
    del _L0_ffn_all
    return {'x': x, 'ctx_2048': ctx_2048, 'g_xattn': g_xattn, 'g_ffn': g_ffn, 'L0_xattn_time_decay': _L0_xattn_in['time_decay'], 'L0_xattn_time_first': _L0_xattn_in['time_first'], 'L0_ffn_conv_w': _L0_ffn_in['conv_w'], 'L0_ffn_Wq': _L0_ffn_in['Wq'], 'L0_ffn_Wk': _L0_ffn_in['Wk'], 'L0_ffn_Wv': _L0_ffn_in['Wv'], 'L0_ffn_Wg': _L0_ffn_in['Wg'], 'L0_ffn_router_w': _L0_ffn_in['router_w'], 'L0_ffn_Wout': _L0_ffn_in['Wout']}

def reference(x, ctx_2048, g_xattn, g_ffn, L0_xattn_time_decay, L0_xattn_time_first, L0_ffn_conv_w, L0_ffn_Wq, L0_ffn_Wk, L0_ffn_Wv, L0_ffn_Wg, L0_ffn_router_w, L0_ffn_Wout):
    import jax
    import jax.numpy as jnp

    def _L0_xattn_ref(batch_size, seq_len, embedding_dim, time_decay, time_first, k, v):
        import jax, jax.numpy as jnp
        import numpy as np

        def _wkv(time_decay, time_first, k, v):
            w = -jnp.exp(time_decay)
            u = time_first
            B, T, C = k.shape
            aa = jnp.zeros((B, C), dtype=k.dtype)
            bb = jnp.zeros((B, C), dtype=k.dtype)
            pp = jnp.full((B, C), -1e+38, dtype=k.dtype)

            def step(carry, kv_t):
                aa, bb, pp = carry
                kt, vt = kv_t
                ww = u + kt
                q = jnp.maximum(pp, ww)
                e1 = jnp.exp(pp - q)
                e2 = jnp.exp(ww - q)
                y_t = (e1 * aa + e2 * vt) / (e1 * bb + e2)
                ww2 = pp + w
                q2 = jnp.maximum(ww2, kt)
                e1b = jnp.exp(ww2 - q2)
                e2b = jnp.exp(kt - q2)
                new_carry = (e1b * aa + e2b * vt, e1b * bb + e2b, q2)
                return (new_carry, y_t)
            ks = jnp.transpose(k, (1, 0, 2))
            vs = jnp.transpose(v, (1, 0, 2))
            _, ys = jax.lax.scan(step, (aa, bb, pp), (ks, vs))
            return jnp.transpose(ys, (1, 0, 2))
        assert seq_len <= 512
        return _wkv(time_decay, time_first, k, v)

    def _L0_ffn_ref(x, conv_w, Wq, Wk, Wv, Wg, router_w, Wout):
        import jax, jax.numpy as jnp
        import numpy as np
        L, B, D = (1024, 1, 1024)
        H = 16
        DK, DV = (D // 2, D)
        HDK, HDV = (DK // H, DV // H)
        RATIO = 2
        BASE = 10000.0
        EPS = 1e-05

        def _apply_rotary(x, cos, sin):
            d2 = x.shape[-1] // 2
            x1, x2 = (x[..., :d2], x[..., d2:])
            return jnp.concatenate([x1 * cos - x2 * sin, x2 * cos + x1 * sin], axis=-1)
        x = jnp.transpose(x, (1, 0, 2))
        b, l, d = x.shape
        x_prev = jnp.pad(x, ((0, 0), (1, 0), (0, 0)))[:, :l]
        x = jax.nn.silu(x_prev * conv_w[:, 0] + x * conv_w[:, 1])
        q = jax.nn.silu(x @ Wq)
        k = x @ Wk
        v = x @ Wv
        g = x @ Wg
        q = q.reshape(b, l, H, HDK).transpose(0, 2, 1, 3)
        k = k.reshape(b, l, H, HDK).transpose(0, 2, 1, 3)
        v = v.reshape(b, l, H, HDV).transpose(0, 2, 1, 3)
        inv_freq = 1.0 / BASE ** (jnp.arange(0, HDK, 2, dtype=jnp.float32) / HDK)
        freqs = jnp.arange(l, dtype=jnp.float32)[:, None] * inv_freq[None, :]
        cos, sin = (jnp.cos(freqs), jnp.sin(freqs))
        q = _apply_rotary(q, cos, sin)
        k = _apply_rotary(k, cos, sin)
        logits = jnp.einsum('bhld,hdr->bhlr', v, router_w)
        scores = jax.nn.softmax(logits, axis=-1)
        onehot = jax.nn.one_hot(jnp.argmax(scores, axis=-1), RATIO, dtype=scores.dtype)
        masked_scores = scores * onehot
        masked_ind = onehot
        sum_ind = jnp.cumsum(masked_ind, axis=2)
        norm = jnp.where(sum_ind > 0, 1.0 / jnp.maximum(sum_ind, 1.0), 0.0)[..., None]
        q_exp = q[:, :, :, None, :] * masked_scores[..., None] * norm
        k_exp = k[:, :, :, None, :] * masked_ind[..., None]
        q_exp = q_exp.reshape(b, H, l, RATIO * HDK)
        k_exp = k_exp.reshape(b, H, l, RATIO * HDK)
        qk = jnp.einsum('bhld,bhmd->bhlm', q_exp, k_exp) * HDK ** (-0.5)
        mask = jnp.tril(jnp.ones((l, l), dtype=qk.dtype))
        qk = qk * mask
        o = jnp.einsum('bhlm,bhmd->bhld', qk, v)
        o = o.transpose(0, 2, 1, 3)
        mu = jnp.mean(o, axis=-1, keepdims=True)
        var = jnp.var(o, axis=-1, keepdims=True)
        o = (o - mu) / jnp.sqrt(var + EPS)
        out = jax.nn.silu(g) * o.reshape(b, l, d)
        out = out @ Wout
        return jnp.transpose(out, (1, 0, 2))
    x = x + jnp.tanh(g_xattn[0]) * _L0_xattn_ref(8, 512, 1024, L0_xattn_time_decay, L0_xattn_time_first, _layernorm(x, axis=-1), ctx_2048)
    x = x + jnp.tanh(g_ffn[0]) * _L0_ffn_ref(_layernorm(x, axis=-1), L0_ffn_conv_w, L0_ffn_Wq, L0_ffn_Wk, L0_ffn_Wv, L0_ffn_Wg, L0_ffn_router_w, L0_ffn_Wout)
    return x

_drawn_inputs = setup_inputs


def setup_inputs(seed=0):
    import zlib

    import numpy as np

    out = dict(_drawn_inputs(seed))
    spreads = {}
    factors = {}
    for name, (base, spread) in spreads.items():
        noise = np.random.default_rng([zlib.crc32(name.encode()), seed]).standard_normal(out[name].shape)
        drawn = base * np.exp(spread * noise) if base else spread * noise
        out[name] = jnp.asarray(drawn.astype(out[name].dtype))
    for name, factor in factors.items():
        out[name] = (out[name] * factor).astype(out[name].dtype)
    return out
```

```python
from contextlib import ExitStack

import concourse.bass as bass
from concourse import mybir

F32 = mybir.dt.float32
F16 = mybir.dt.float16
ALU = mybir.AluOpType
ACT = mybir.ActivationFunctionType
AX_X = mybir.AxisListType.X
AMAX = bass.bass_isa.ReduceOp.max

P = 128
NB = 8
TT = P // NB
SEG = TT + 1
C = 1024
KC = C // P
HALF = C // 2
H = 16
DK = 32
DV = 64
HG = 4
NG = H // HG
EPS = 1e-5
SHIFT = 40.0
U_MAX = 87.0
TINY = 1e-30
LN_BOUND = float(C) ** 0.5
HEAD_BOUND = float(DV) ** 0.5
W_TOP = 2.0 ** 14
H_TOP = 2.0 ** 15
G_TOP = 2.0 ** 14
UNITS = ("q", "k", "v0", "v1", "g0", "g1", "o0", "o1")
UQ, UK, UV, UG, UO = 0, 1, 2, 4, 6


def flamingo_layer(nc, x, ctxt, g_xattn, g_ffn, decay_cols, first_cols, conv_cols, w_q, w_k, w_v, w_g,
                   router, w_out, identity, causal, cos_rows, sin_rows, count_rows, head_rows, out):
    T = x.shape[1]
    N = T // TT
    LOOPED = (N - 3) // 3 * 3
    x_t = x.rearrange("b t c -> t b c")
    v_t = ctxt.rearrange("b t c -> t b c")
    out_t = out.rearrange("b t c -> t b c")
    w_src = [w_q, w_k, w_v[:, 0:HALF], w_v[:, HALF:C], w_g[:, 0:HALF], w_g[:, HALF:C],
             w_out[:, 0:HALF], w_out[:, HALF:C]]

    with ExitStack() as ctx:
        def sb(name, shape, dt=F32):
            return ctx.enter_context(nc.sbuf_tensor(name, shape, dt))

        def bank(name):
            return ctx.enter_context(nc.psum_tensor(name, [P, HALF], F32))

        def sem(name):
            return ctx.enter_context(nc.semaphore(name))

        w_hi = sb("w_hi", [P, len(UNITS), KC, HALF], F16)
        w_lo = sb("w_lo", [P, len(UNITS), KC, HALF], F16)
        x_ring = sb("x_ring", [P, 3, C])
        vx = sb("vx", [P, C])
        ek = sb("ek", [P, C])
        decay = sb("decay", [P, KC * NB * SEG])
        seg = sb("seg", [P, KC * NB * SEG])
        fa = sb("fa", [P, C])
        fb = sb("fb", [P, C])
        h_hi = sb("h_hi", [P, C], F16)
        h_lo = sb("h_lo", [P, C], F16)
        work = sb("work", [P, 2, KC * HALF])
        v2 = work[:, 0, 0:2 * C].rearrange("p (h s d) -> p h s d", h=H, s=2)
        sg = work[:, 0, 2 * C:3 * C]
        o_sb = work[:, 0, 3 * C:4 * C]
        q_sb = work[:, 1, 0:HALF]
        k_sb = work[:, 1, HALF:C]
        rot_q = work[:, 1, C:C + HALF]
        rot_k = work[:, 1, C + HALF:2 * C]
        probs = (rot_q, rot_k)
        g_split = work[:, 1, 2 * C:3 * C].bitcast(F16)
        gt_hi, gt_lo = g_split[:, 0:C], g_split[:, C:2 * C]
        q_blk = (work[:, 1, 2 * C:2 * C + HALF], work[:, 1, 2 * C + HALF:3 * C])
        squares = work[:, 1, 2 * C:3 * C]
        tmp = work[:, 1, 3 * C:4 * C]
        router_d = sb("router_d", [P, C])
        ident = sb("ident", [P, P])
        causal_m = sb("causal_m", [P, P])
        cos2 = sb("cos2", [P, DK])
        sin2 = sb("sin2", [P, DK])
        cnt_c = sb("cnt_c", [P, 1])
        head_m = sb("head_m", [P, HG])
        small = sb("small", [P, 360])
        at = [0]

        def col(n):
            at[0] += n
            return small[:, at[0] - n:at[0]]

        dk = col(KC)
        eu = col(KC)
        cw0, cw1 = col(KC), col(KC)
        mx = col(len(UNITS) + 1)
        sw = col(len(UNITS) + 1)
        inv = col(len(UNITS))
        tg = col(2)
        base = col(2)
        nhalf = col(H)
        eps_c, dv_c = col(H), col(H)
        shift1, shift2 = col(1), col(1)
        st1, st2 = col(12), col(12)
        mv1, mv2 = col(2), col(2)
        ve1, ve2 = col(1), col(1)
        rs1, rs2 = col(1), col(1)
        nm1, nm2 = col(1), col(1)
        nb1, nb2 = col(1), col(1)
        delta = col(H)
        sgn = col(H)
        pr = col(H)
        coef = col(H)
        ctmp = col(H)
        osum = col(H)
        ossq = col(H)
        ftmp = col(H)
        fac = col(H)
        gmx = col(1)
        grc = col(1)
        gsc = col(1)
        usc = col(2)
        carry_b = sb("carry_b", [P, KC * NB])
        carry_a = sb("carry_a", [P, KC * NB])

        ps_t = (bank("ps_t0"), bank("ps_t1"))
        ps_g = (bank("ps_g0"), bank("ps_g1"))
        ps_s = (bank("ps_s0"), bank("ps_s1"))
        ps_o = (bank("ps_o0"), bank("ps_o1"))

        s_const, s_w = sem("const_loaded"), [sem(f"weight_loaded{n}") for n in range(2)]
        s_x, s_vl, s_store = sem("x_loaded"), sem("v_loaded"), sem("out_stored")
        s_wmax, s_wall, s_wsc, s_whi, s_wlo = (sem(n) for n in
            ("wmax_done", "wmax_all", "wscale_done", "whi_done", "wlo_done"))
        s_ca, s_cv, s_cp = sem("const_act"), sem("const_dve"), sem("const_pool")
        s_etp, s_evp, s_yp, s_xnp = sem("ek_transposed"), sem("ev_transposed"), sem("y_transposed"), sem("xn_transposed")
        s_qp, s_kp, s_vp, s_gp, s_up = sem("q_proj"), sem("k_proj"), sem("v_proj"), sem("g_proj"), sem("out_proj")
        s_qtp, s_ktp, s_gtp = sem("q_transposed"), sem("k_transposed"), sem("gated_transposed")
        s_cump, s_sp, s_op = sem("cum_matmul"), sem("scores_matmul"), sem("o_matmul")
        s_bn1, s_ag1, s_rs1, s_nb1, s_e, s_ev = (sem(n) for n in
            ("bn1", "aggr1", "rstd1", "nbias1", "ek_done", "ev_done"))
        s_sega, s_segb = sem("seg_den_copied"), sem("seg_num_copied")
        s_fda, s_fdb = sem("first_den"), sem("first_num")
        s_sca, s_scb, s_sva, s_svb = sem("scan_den"), sem("scan_num"), sem("save_den"), sem("save_num")
        s_den, s_num, s_rec, s_y, s_x2 = (sem(n) for n in
            ("den_done", "num_done", "recip_done", "y_done", "x2_done"))
        s_bn2, s_ag2, s_rs2, s_nb2, s_xn = (sem(n) for n in
            ("bn2", "aggr2", "rstd2", "nbias2", "xn_done"))
        s_z, s_z2, s_pre, s_h, s_hhi, s_hlo = (sem(n) for n in
            ("conv_now", "conv_past", "conv_done", "h_done", "h_hi_done", "h_lo_done"))
        s_q, s_k, s_vc = sem("q_copied"), sem("k_copied"), sem("v_copied")
        s_r1q, s_r1k, s_rq, s_rk = sem("rot_q_part"), sem("rot_k_part"), sem("rot_q"), sem("rot_k")
        s_qt, s_kt = sem("qt_copied"), sem("kt_copied")
        s_vr, s_dl = sem("v_router"), sem("delta_done")
        s_sgn, s_sv, s_th, s_pr, s_cum, s_cf = (sem(n) for n in
            ("sign_done", "signed_v", "tanh_done", "prob_done", "cum_done", "coef_done"))
        s_sm = sem("dve_small")
        s_qb, s_p, s_ob, s_o = sem("q_block"), sem("probs_done"), sem("o_part"), sem("o_done")
        s_os, s_oc, s_sq, s_ss = sem("o_sum"), sem("o_centred"), sem("o_square"), sem("o_var")
        s_os2 = sem("o_mean")
        s_fp, s_f, s_og, s_gt = sem("factor_part"), sem("factor"), sem("o_times_gate"), sem("gated")
        s_gthi, s_gtlo = sem("gt_hi"), sem("gt_lo")
        s_sg, s_gm, s_gm2, s_gs, s_us = (sem(n) for n in
            ("silu_g", "gate_max", "gate_max_guard", "gate_scale", "out_scale"))
        s_fin = sem("final_done")
        s_rg, s_y0 = sem("gate_recip"), sem("first_step_state")

        block = ctx.enter_context(nc.Block())

        def seg4(lo, hi):
            return seg[:, :].rearrange("p (c b t) -> p c t b", c=KC, b=NB)[:, :, lo:hi, :]

        seg_rows = seg[:, :].rearrange("p (s t) -> p s t", t=SEG)

        def tok(ap):
            return ap.rearrange("p (c t b) -> p c t b", t=TT, b=NB)

        def per_chunk(cols, lo, hi, n):
            return cols[:, lo:hi].rearrange("p (c o) -> p c o", o=1).to_broadcast([P, hi - lo, n])

        def per_head(cols, lo, hi, n):
            return cols[:, lo:hi].rearrange("p (h o) -> p h o", o=1).to_broadcast([P, hi - lo, n])

        def by_head(ap, d):
            return ap.rearrange("p (h d) -> p h d", d=d)

        def after(eng, s, value):
            if not isinstance(value, int) or value > 0:
                eng.wait_ge(s, value)

        def pipeline(eng, step):
            step(-2, 1, False, False, True, False)
            step(-1, 2, False, True, True, False)
            step(0, 0, True, True, True, False)
            with eng.Fori(1, LOOPED + 1, 3) as i:
                for r in range(3):
                    step(i + r, (1 + r) % 3, True, True, True, True)
            for i in range(LOOPED + 1, N - 2):
                step(i, i % 3, True, True, True, True)
            step(N - 2, (N - 2) % 3, True, True, False, True)
            step(N - 1, (N - 1) % 3, True, False, False, True)
            step(N, N % 3, False, False, False, True)

        def rotate(eng, E, i, half_of_tmp, src, dst, parts, done):
            scratch = tmp[:, half_of_tmp * HALF:(half_of_tmp + 1) * HALF]
            s4 = src.rearrange("p (h s d) -> p h s d", h=H, s=2)
            t4 = scratch.rearrange("p (h s d) -> p h s d", h=H, s=2)
            half = DK // 2
            E.tensor_tensor(by_head(dst, DK), by_head(src, DK),
                            cos2[:, :].rearrange("p (o d) -> p o d", o=1).to_broadcast([P, H, DK]), ALU.mult)\
             .then_inc(parts, 1)
            for s in range(2):
                E.tensor_tensor(t4[:, :, s, :], s4[:, :, 1 - s, :],
                                sin2[:, s * half:(s + 1) * half].rearrange("p (o d) -> p o d", o=1)
                                .to_broadcast([P, H, half]), ALU.mult).then_inc(parts, 1)
            eng.wait_ge(parts, 3 * (i + 1))
            E.tensor_tensor(dst, dst, scratch, ALU.add).then_inc(done, 1)

        @block.sync
        def _(sp):
            def load_x(j, slot):
                sp.dma_start(x_ring[:, slot, :], x_t[bass.ds(j * TT, TT), :, :]).then_inc(s_x, 16)

            def load_v(j):
                sp.dma_start(vx[:, :], v_t[bass.ds(j * TT, TT), :, :]).then_inc(s_vl, 16)

            def load_unit(u):
                if u >= 2:
                    after(sp, s_whi, u - 1)
                    after(sp, s_wlo, u - 1)
                sp.dma_start(work[:, u % 2, :].rearrange("p (k n) -> p k n", k=KC),
                             w_src[u].rearrange("(k p) n -> p k n", p=P)).then_inc(s_w[u % 2], 16)

            load_x(0, 0)
            load_v(0)
            for dst, src in ((dk, decay_cols), (eu, first_cols), (cw0, conv_cols[0]), (cw1, conv_cols[1]),
                             (ident[:, :], identity), (causal_m[:, :], causal), (cos2[:, :], cos_rows),
                             (sin2[:, :], sin_rows), (cnt_c[:, :], count_rows), (head_m[:, :], head_rows),
                             (tg[:, 0:1], g_xattn.to_broadcast([P, 1])), (tg[:, 1:2], g_ffn.to_broadcast([P, 1])),
                             (router_d[:, :], router[0:1, :].to_broadcast([P, C])),
                             (fb[:, :], router[1:2, :].to_broadcast([P, C]))):
                sp.dma_start(dst, src).then_inc(s_const, 16)
            load_unit(0)
            load_unit(1)
            load_x(1, 1)
            for u in range(2, len(UNITS)):
                load_unit(u)

            def step(i, slot, main, nxt, nxt2, prev):
                if prev:
                    after(sp, s_fin, 2 * i)
                    sp.dma_start(out_t[bass.ds((i - 1) * TT, TT), :, :], x_ring[:, (slot + 2) % 3, :])\
                      .then_inc(s_store, 16)
                if nxt2 and (not isinstance(i, int) or i >= 0):
                    after(sp, s_store, 16 * i)
                    load_x(i + 2, (slot + 2) % 3)
                if nxt2 and (not isinstance(i, int) or i >= -1):
                    after(sp, s_xnp, 2 * (i + 2))
                    load_v(i + 2)

            pipeline(sp, step)
            sp.wait_ge(s_store, 16 * N)

        @block.tensor
        def _(pe):
            def transposes(dst, src, s):
                for n in range(4):
                    last = nc.tensor.transpose(dst[:, n * P:(n + 1) * P], src[:, n * P:(n + 1) * P], ident[:, :])
                last.then_inc(s, 1)

            def project(dst, a_hi, a_lo, u, s, part=None):
                for kc in range(KC) if part is None else range(part * KC // 2, (part + 1) * KC // 2):
                    hi, lo = (a[:, kc * P:(kc + 1) * P] for a in (a_hi, a_lo))
                    nc.tensor.matmul(dst[:, :], hi, w_hi[:, u, kc, :], start=(kc == 0), stop=False)
                    nc.tensor.matmul(dst[:, :], hi, w_lo[:, u, kc, :], start=False, stop=False)
                    last = nc.tensor.matmul(dst[:, :], lo, w_hi[:, u, kc, :], start=False, stop=(kc == KC - 1))
                if part != 0:
                    last.then_inc(s, 1)

            def step(i, slot, main, nxt, nxt2, prev):
                n, p = i + 1, i - 1
                if main:
                    after(pe, s_hlo, 2 * i + 1)
                    after(pe, s_sg, 2 * i - 1)
                    project(ps_g[0], h_hi, h_lo, UQ, s_qp, 0)
                if nxt:
                    for g in range(2):
                        after(pe, s_e, n + 1)
                        after(pe, s_z, 2 * n)
                        after(pe, s_z2, 2 * n)
                        transposes(ps_t[g], ek[:, g * HALF:(g + 1) * HALF], s_etp)
                if main:
                    after(pe, s_hlo, 2 * (i + 1))
                    project(ps_g[0], h_hi, h_lo, UQ, s_qp, 1)
                    after(pe, s_sg, 2 * i)
                    project(ps_g[1], h_hi, h_lo, UK, s_kp, 0)
                if nxt:
                    for g in range(2):
                        after(pe, s_ev, n + 1)
                        after(pe, s_fda, 2 * n + g + 1)
                        transposes(ps_t[g], vx[:, g * HALF:(g + 1) * HALF], s_evp)
                if main:
                    project(ps_g[1], h_hi, h_lo, UK, s_kp, 1)
                    after(pe, s_q, i + 1)
                    project(ps_g[0], h_hi, h_lo, UV, s_vp)
                    for g in range(2):
                        after(pe, (s_rq, s_rk)[g], i + 1)
                        if nxt:
                            after(pe, s_fdb, 2 * n + g + 1)
                        elif g == 0:
                            after(pe, s_z, 2 * (i + 1))
                            after(pe, s_z2, 2 * (i + 1))
                        transposes(ps_t[g], (rot_q, rot_k)[g], (s_qtp, s_ktp)[g])
                    after(pe, s_k, i + 1)
                    project(ps_g[1], h_hi, h_lo, UV + 1, s_vp, 0)
                if prev:
                    for g in range(2):
                        after(pe, s_gt, p + 1)
                        if main:
                            after(pe, (s_qt, s_kt)[g], i + 1)
                        else:
                            after(pe, s_gtlo, 2 * p)
                        transposes(ps_t[g], o_sb[:, g * HALF:(g + 1) * HALF], s_gtp)
                if main:
                    project(ps_g[1], h_hi, h_lo, UV + 1, s_vp, 1)
                if prev:
                    for g in range(2):
                        if main:
                            after(pe, s_vc, 2 * i + g + 1)
                        else:
                            after(pe, s_sg, 2 * p + g + 1)
                        for part in range(2):
                            if g == 0:
                                after(pe, s_gtlo, 2 * p + part + 1)
                            project(ps_g[g], gt_hi, gt_lo, UO + g, s_up, part)
                            if nxt and (g, part) == (0, 0):
                                y_transposes(n, p, prev)
                elif nxt:
                    y_transposes(n, p, prev)
                if main:
                    after(pe, s_sgn, i + 1)
                    after(pe, s_p, 4 * i)
                    nc.tensor.matmul(ps_s[0][:, 0:H], causal_m[:, :], sgn, start=True, stop=True)\
                      .then_inc(s_cump, 1)
                if nxt:
                    for g in range(2):
                        after(pe, s_xn, n + 1)
                        after(pe, s_x2, 2 * n + g + 1)
                        transposes(ps_t[g], vx[:, g * HALF:(g + 1) * HALF], s_xnp)
                if main:
                    for g in range(2):
                        if prev:
                            after(pe, s_fin, 2 * p + g + 1)
                        else:
                            after(pe, s_vc, 2 * i + g + 1)
                        for part in range(2):
                            project(ps_g[g], h_hi, h_lo, UG + g, s_gp, part)
                            if (g, part) == (0, 0):
                                scores(i, 0)
                                scores(i, 1)
                            elif (g, part) != (1, 1):
                                values(i, g)
                                scores(i, g + 2)
                    values(i, 2)
                    values(i, 3)

            def y_transposes(n, p, prev):
                for g in range(2):
                    after(pe, s_y, n + 1)
                    after(pe, s_fdb, 2 * n + g + 1)
                    if prev:
                        after(pe, s_gtlo, 2 * p + g + 1)
                    elif not isinstance(n, int) or n >= 1:
                        after(pe, (s_qt, s_kt)[g], n)
                    transposes(ps_t[g], fb[:, g * HALF:(g + 1) * HALF], s_yp)

            def scores(i, g):
                after(pe, s_qb, 4 * i + g + 1)
                after(pe, s_kt, i + 1)
                after(pe, s_p, 4 * i + g - 1)
                if g == 0:
                    after(pe, s_cum, i + 1)
                nc.tensor.matmul(ps_s[g % 2][:, :], k_sb[:, g * P:(g + 1) * P], q_blk[g % 2],
                                 start=True, stop=True).then_inc(s_sp, 1)

            def values(i, g):
                after(pe, s_p, 4 * i + g + 1)
                after(pe, s_sv, i + 1)
                after(pe, s_o, 4 * i + g - 1)
                for h in range(HG):
                    last = nc.tensor.matmul(ps_o[g % 2][:, h * P:(h + 1) * P], probs[g % 2][:, h * P:(h + 1) * P],
                                            v2[:, g * HG + h, :, :].rearrange("p s d -> p (s d)"),
                                            start=True, stop=True)
                last.then_inc(s_op, 1)

            pe.wait_ge(s_const, 16 * 14)
            pipeline(pe, step)

        @block.scalar
        def _(act):
            A = nc.scalar.activation
            act.wait_ge(s_const, 16 * 14)
            A(dk, dk, ACT.Exp).then_inc(s_ca, 1)
            act.wait_ge(s_ca, 1)
            A(dk, dk, ACT.Exp, scale=-1.0).then_inc(s_ca, 1)
            act.wait_ge(s_cv, 1)
            A(eu, eu, ACT.Exp).then_inc(s_ca, 1)
            A(tg, tg, ACT.Tanh).then_inc(s_ca, 1)
            A(delta[:, 0:KC], cw0, ACT.Abs).then_inc(s_ca, 1)
            A(sgn[:, 0:KC], cw1, ACT.Abs).then_inc(s_ca, 1)

            def split_unit(u):
                act.wait_ge(s_wsc, u + 1)
                A(w_hi[:, u, :, :].rearrange("p k n -> p (k n)"), work[:, u % 2, :], ACT.Copy,
                  scale=sw[:, u:u + 1]).then_inc(s_whi, 1)

            def exp_k(j, slot):
                act.wait_ge(s_nb1, j + 1)
                after(act, s_etp, 2 * j)
                A(ek[:, :], x_ring[:, slot, :], ACT.Exp, scale=rs1, bias=nb1).then_inc(s_e, 1)

            def fill_segments(j, ps_sem, carry, saved, free, free_at, done):
                after(act, free, free_at)
                after(act, saved, j)
                A(seg_rows[:, :, 0], carry[:, :], ACT.Copy).then_inc(done, 1)
                for g in range(2):
                    act.wait_ge(ps_sem, 2 * j + g + 1)
                    A(seg4(1, SEG)[:, g * 4:(g + 1) * 4, :, :], tok(ps_t[g][:, :]), ACT.Copy).then_inc(done, 1)

            def step(i, slot, main, nxt, nxt2, prev):
                n, p = i + 1, i - 1
                if prev:
                    after(act, s_oc, p + 1)
                    after(act, s_sp, 4 * (p + 1))
                    A(squares, o_sb, ACT.Square).then_inc(s_sq, 1)
                if nxt:
                    fill_segments(n, s_etp, carry_b, s_sva, s_pre, n, s_sega)
                if main:
                    if isinstance(i, int) and i == 0:
                        act.wait_ge(s_wlo, len(UNITS))
                    act.wait_ge(s_qp, i + 1)
                    after(act, s_qb, 4 * i)
                    A(q_sb, ps_g[0][:, :], ACT.Silu, scale=inv[:, UQ:UQ + 1]).then_inc(s_q, 1)
                    if nxt:
                        fill_numerator(n)
                    act.wait_ge(s_kp, i + 1)
                    after(act, s_sp, 4 * i)
                    A(k_sb, ps_g[1][:, :], ACT.Copy, scale=inv[:, UK:UK + 1]).then_inc(s_k, 1)
                elif nxt:
                    fill_numerator(n)
                if main:
                    copy_v(i, 0)
                    act.wait_ge(s_qtp, i + 1)
                    A(q_sb, ps_t[0][:, :], ACT.Copy).then_inc(s_qt, 1)
                    act.wait_ge(s_ktp, i + 1)
                    A(k_sb, ps_t[1][:, :], ACT.Copy).then_inc(s_kt, 1)
                if prev:
                    for g in range(2):
                        act.wait_ge(s_gtp, 2 * p + g + 1)
                        act.wait_ge(s_ss, p + 1)
                        A(gt_hi[:, g * HALF:(g + 1) * HALF], ps_t[g][:, :], ACT.Copy).then_inc(s_gthi, 1)
                if main:
                    copy_v(i, 1)
                    act.wait_ge(s_dl, 2 * (i + 1))
                    after(act, s_cf, i)
                    A(pr, delta, ACT.Abs).then_inc(s_th, 1)
                    act.wait_ge(s_th, 2 * i + 1)
                    A(pr, pr, ACT.Tanh, scale=0.5).then_inc(s_th, 1)
                if nxt:
                    act.wait_ge(s_nb2, n + 1)
                    act.wait_ge(s_evp, 2 * n + 2)
                    A(vx[:, :], x_ring[:, (slot + 1) % 3, :], ACT.Identity, scale=rs2, bias=nb2).then_inc(s_xn, 1)
                if main:
                    silu_gate(i, 0)
                if nxt:
                    act.wait_ge(s_pre, n + 1)
                    A(fa[:, :], fa[:, :], ACT.Silu).then_inc(s_h, 1)
                if main:
                    silu_gate(i, 1)
                if nxt:
                    act.wait_ge(s_h, n + 1)
                    after(act, s_gp, 2 * (i + 1) if main else 0)
                    for g in range(2):
                        A(h_hi[:, g * HALF:(g + 1) * HALF], fa[:, g * HALF:(g + 1) * HALF], ACT.Copy,
                          scale=sw[:, len(UNITS):len(UNITS) + 1]).then_inc(s_hhi, 1)
                if nxt2:
                    exp_k(i + 2, (slot + 2) % 3)

            def fill_numerator(n):
                act.wait_ge(s_sva, n + 1)
                fill_segments(n, s_evp, carry_a, s_svb, s_den, n + 1, s_segb)

            def silu_gate(i, g):
                act.wait_ge(s_gp, 2 * i + g + 1)
                after(act, s_og, i)
                after(act, s_gm, i)
                A(sg[:, g * HALF:(g + 1) * HALF], ps_g[g][:, :], ACT.Silu,
                  scale=inv[:, UG + g:UG + g + 1]).then_inc(s_sg, 1)

            def copy_v(i, g):
                act.wait_ge(s_vp, 2 * i + g + 1)
                after(act, s_op, 4 * i)
                A(v2[:, g * 8:(g + 1) * 8, 0, :], by_head(ps_g[g][:, :], DV), ACT.Copy,
                  scale=inv[:, UV + g:UV + g + 1]).then_inc(s_vc, 1)

            for u in range(len(UNITS)):
                split_unit(u)
            pipeline(act, step)

        @block.vector
        def _(dve):
            V = nc.vector
            dve.wait_ge(s_const, 16 * 14)
            V.tensor_scalar(eu, eu, U_MAX, None, ALU.min).then_inc(s_cv, 1)
            V.tensor_tensor(router_d[:, :], router_d[:, :], fb[:, :], ALU.subtract).then_inc(s_cv, 1)
            for cols, value in ((nhalf, -0.5), (eps_c, EPS), (dv_c, 1.0 / DV), (shift1, -SHIFT), (shift2, 0.0)):
                V.memset(cols, value).then_inc(s_cv, 1)
            V.memset(carry_a[:, :], 0.0).then_inc(s_cv, 1)
            V.memset(carry_b[:, :], 0.0).then_inc(s_cv, 1)
            V.memset(decay[:, :], 0.0).then_inc(s_cv, 1)
            dve.wait_ge(s_cv, 10)
            dve.wait_ge(s_ca, 6)
            V.tensor_copy(decay[:, :].rearrange("p (c b t) -> p c b t", c=KC, b=NB)[:, :, :, 1:SEG],
                          dk.rearrange("p (c o q) -> p c o q", o=1, q=1).to_broadcast([P, KC, NB, TT]))\
             .then_inc(s_cv, 1)
            V.tensor_tensor(delta[:, 0:KC], delta[:, 0:KC], sgn[:, 0:KC], ALU.add).then_inc(s_cv, 1)
            dve.wait_ge(s_cv, 12)
            U = len(UNITS)
            V.tensor_reduce(mx[:, U:U + 1], delta[:, 0:KC], AX_X, ALU.max).then_inc(s_wmax, 1)

            def scale_of(u, top, count):
                dve.wait_ge(s_wall, count)
                V.tensor_scalar(mx[:, u:u + 1], mx[:, u:u + 1], TINY, None, ALU.max).then_inc(s_sm, 1)
                dve.wait_ge(s_sm, 3 * count - 2)
                V.reciprocal(sw[:, u:u + 1], mx[:, u:u + 1]).then_inc(s_sm, 1)
                dve.wait_ge(s_sm, 3 * count - 1)
                V.tensor_scalar(sw[:, u:u + 1], sw[:, u:u + 1], top, None, ALU.mult).then_inc(s_sm, 1)
                dve.wait_ge(s_sm, 3 * count)

            def max_unit(u):
                dve.wait_ge(s_w[u % 2], 16 * (u // 2 + 1))
                V.tensor_reduce(mx[:, u:u + 1], work[:, u % 2, :], AX_X, ALU.max,
                                apply_absolute_value=True).then_inc(s_wmax, 1)

            def lo_unit(u):
                dve.wait_ge(s_whi, u + 1)
                V.scalar_tensor_tensor(w_lo[:, u, :, :].rearrange("p k n -> p (k n)"), work[:, u % 2, :],
                                       sw[:, u:u + 1], w_hi[:, u, :, :].rearrange("p k n -> p (k n)"),
                                       ALU.mult, ALU.subtract).then_inc(s_wlo, 1)

            scale_of(U, H_TOP / LN_BOUND, 1)
            for u in range(U):
                max_unit(u)
                if u:
                    lo_unit(u - 1)
                scale_of(u, W_TOP, u + 2)
                V.tensor_scalar(inv[:, u:u + 1], mx[:, u:u + 1], mx[:, U:U + 1],
                                LN_BOUND / (W_TOP * H_TOP), ALU.mult, ALU.mult).then_inc(s_wsc, 1)
            lo_unit(U - 1)
            for g in range(2):
                V.tensor_scalar(base[:, g:g + 1], mx[:, UO + g:UO + g + 1], tg[:, 1:2], 1.0 / W_TOP,
                                ALU.mult, ALU.mult).then_inc(s_cv, 1)
            dve.wait_ge(s_cv, 14)

            def norm_stats(j, src, st, mv, s_bn, s_ag):
                after(dve, s_ag, j)
                for g in range(2):
                    last = V.bn_stats(st[:, 6 * g:6 * g + 6], src[:, g * HALF:(g + 1) * HALF])
                last.then_inc(s_bn, 1)
                dve.wait_ge(s_cv, 14)
                dve.wait_ge(s_bn, j + 1)
                V.bn_aggr(mv, st).then_inc(s_ag, 1)

            def recurrence_terms(n, done, dst, first):
                for g in range(2):
                    dve.wait_ge(done, 3 * n + g + 2)
                    V.tensor_tensor(dst[:, g * HALF:(g + 1) * HALF].rearrange("p (c n) -> p c n", n=P),
                                    ps_t[g][:, :].rearrange("p (c n) -> p c n", n=P),
                                    per_chunk(eu, 4 * g, 4 * g + 4, P), ALU.mult).then_inc(first, 1)

            def scan(n, scanned, carry, saved):
                V.tensor_tensor_scan(seg[:, :], decay[:, :], seg[:, :], 0.0, ALU.mult, ALU.add).then_inc(scanned, 1)
                dve.wait_ge(scanned, n + 1)
                V.tensor_copy(carry[:, :], seg_rows[:, :, TT]).then_inc(saved, 1)
                if isinstance(n, int) and n == 0:
                    V.tensor_copy(seg_rows[:, :, 0], seg_rows[:, :, 1]).then_inc(s_y0, 1)
                    dve.wait_ge(s_y0, 1 if carry is carry_b else 2)

            def add_state(dst, done):
                V.tensor_tensor(tok(dst), tok(dst), seg4(0, TT), ALU.add).then_inc(done, 1)

            def step(i, slot, main, nxt, nxt2, prev):
                n, p = i + 1, i - 1
                o_h = by_head(o_sb, DV)
                if prev:
                    dve.wait_ge(s_o, 4 * (p + 1))
                    after(dve, s_oc, p)
                    V.tensor_reduce(osum, o_h, AX_X, ALU.add).then_inc(s_os, 1)
                    dve.wait_ge(s_os, p + 1)
                    V.tensor_scalar(osum, osum, 1.0 / DV, None, ALU.mult).then_inc(s_os2, 1)
                    dve.wait_ge(s_os2, p + 1)
                    V.tensor_tensor(o_h, o_h, per_head(osum, 0, H, DV), ALU.subtract).then_inc(s_oc, 1)
                if nxt:
                    after(dve, s_hlo, 2 * n)
                    recurrence_terms(n, s_sega, fa, s_fda)
                    scan(n, s_sca, carry_b, s_sva)
                    dve.wait_ge(s_fda, 2 * n + 2)
                    add_state(fa, s_den)
                if prev:
                    gate_scale(p)
                    dve.wait_ge(s_sq, p + 1)
                    V.tensor_reduce(ossq, by_head(squares, DV), AX_X, ALU.add).then_inc(s_ss, 1)
                if nxt:
                    after(dve, s_yp, 2 * n)
                    recurrence_terms(n, s_segb, fb, s_fdb)
                    scan(n, s_scb, carry_a, s_svb)
                    dve.wait_ge(s_fdb, 2 * n + 2)
                    add_state(fb, s_num)
                if main:
                    dve.wait_ge(s_q, i + 1)
                    after(dve, s_op, 4 * i)
                    after(dve, s_o, 4 * i)
                    rotate(dve, V, i, 0, q_sb, rot_q, s_r1q, s_rq)
                if prev:
                    dve.wait_ge(s_f, p + 1)
                    dve.wait_ge(s_og, p + 1)
                    V.tensor_tensor(o_h, o_h, per_head(fac, 0, H, DV), ALU.mult).then_inc(s_gt, 1)
                if nxt:
                    dve.wait_ge(s_den, n + 1)
                    V.reciprocal(fa[:, :], fa[:, :]).then_inc(s_rec, 1)
                    dve.wait_ge(s_num, n + 1)
                    dve.wait_ge(s_rec, n + 1)
                    V.tensor_tensor(fb[:, :], fb[:, :], fa[:, :], ALU.mult).then_inc(s_y, 1)
                if prev:
                    for g in range(2):
                        dve.wait_ge(s_gthi, 2 * p + g + 1)
                        part = slice(g * HALF, (g + 1) * HALF)
                        V.tensor_tensor(gt_lo[:, part], ps_t[g][:, :], gt_hi[:, part], ALU.subtract)\
                         .then_inc(s_gtlo, 1)
                if main:
                    for g in range(2):
                        dve.wait_ge(s_vr, 2 * i + g + 1)
                        V.tensor_reduce(delta[:, g * 8:(g + 1) * 8], by_head(tmp[:, g * HALF:(g + 1) * HALF], DV),
                                        AX_X, ALU.add).then_inc(s_dl, 1)
                    dve.wait_ge(s_dl, 2 * (i + 1))
                    after(dve, s_sv, i)
                    V.tensor_scalar(sgn, delta, 0.0, 2.0, ALU.is_ge, ALU.mult).then_inc(s_ob, 1)
                    dve.wait_ge(s_ob, 5 * i + 1)
                    V.tensor_scalar(sgn, sgn, -1.0, None, ALU.add).then_inc(s_sgn, 1)
                if nxt:
                    xs = x_ring[:, (slot + 1) % 3, :]
                    for g in range(2):
                        dve.wait_ge(s_yp, 2 * n + g + 1)
                        part = slice(g * HALF, (g + 1) * HALF)
                        V.scalar_tensor_tensor(xs[:, part], ps_t[g][:, :], tg[:, 0:1], xs[:, part],
                                               ALU.mult, ALU.add).then_inc(s_x2, 1)
                    dve.wait_ge(s_x2, 2 * (n + 1))
                    norm_stats(n, xs, st2, mv2, s_bn2, s_ag2)
                if prev:
                    dve.wait_ge(s_us, p + 1)
                    final(p, 0, (slot + 2) % 3)
                if main:
                    dve.wait_ge(s_cump, i + 1)
                    after(dve, s_cf, i)
                    V.tensor_tensor(ctmp, ps_s[0][:, 0:H], sgn, ALU.mult).then_inc(s_cum, 1)
                    dve.wait_ge(s_cum, i + 1)
                    V.tensor_scalar(ctmp, ctmp, cnt_c[:, :], None, ALU.add).then_inc(s_pr, 1)
                    dve.wait_ge(s_pr, 3 * i + 1)
                    V.reciprocal(ctmp, ctmp).then_inc(s_pr, 1)
                    dve.wait_ge(s_th, 2 * (i + 1))
                    V.tensor_scalar(pr, pr, 0.5 * DK ** -0.5, 0.5 * DK ** -0.5, ALU.mult, ALU.add).then_inc(s_pr, 1)
                    dve.wait_ge(s_pr, 3 * (i + 1))
                    V.tensor_tensor(coef, pr, ctmp, ALU.mult).then_inc(s_cf, 1)
                if prev:
                    final(p, 1, (slot + 2) % 3)
                if main:
                    q_block(i, 0)
                    q_block(i, 1)
                if nxt:
                    dve.wait_ge(s_y, n + 1)
                    conv_products(n, 0)
                if main:
                    mask(i, 0)
                    q_block(i, 2)
                if nxt:
                    conv_products(n, 1)
                if main:
                    mask(i, 1)
                    q_block(i, 3)
                if nxt:
                    dve.wait_ge(s_z, 2 * (n + 1))
                    dve.wait_ge(s_z2, 2 * (n + 1))
                    V.tensor_tensor(tok(fa[:, :])[:, :, :, 1:NB], tok(fa[:, :])[:, :, :, 1:NB],
                                    tok(seg[:, 0:C])[:, :, :, 0:NB - 1], ALU.add).then_inc(s_pre, 1)
                if main:
                    head_out(i, 0)
                    mask(i, 2)
                    head_out(i, 1)
                    mask(i, 3)
                if nxt2:
                    first_norm(i + 2, (slot + 2) % 3)
                if nxt:
                    for g in range(2):
                        dve.wait_ge(s_hhi, 2 * n + g + 1)
                        part = slice(g * HALF, (g + 1) * HALF)
                        V.scalar_tensor_tensor(h_lo[:, part], fa[:, part], sw[:, U:U + 1], h_hi[:, part],
                                               ALU.mult, ALU.subtract).then_inc(s_hlo, 1)
                if main:
                    head_out(i, 2)
                    head_out(i, 3)

            def final(p, g, slot):
                part = slice(g * HALF, (g + 1) * HALF)
                dve.wait_ge(s_up, 2 * p + g + 1)
                V.scalar_tensor_tensor(x_ring[:, slot, part], ps_g[g][:, :], usc[:, g:g + 1], x_ring[:, slot, part],
                                       ALU.mult, ALU.add).then_inc(s_fin, 1)

            def conv_products(n, g):
                dve.wait_ge(s_xnp, 2 * n + g + 1)
                V.tensor_tensor(fa[:, g * HALF:(g + 1) * HALF].rearrange("p (c n) -> p c n", n=P),
                                ps_t[g][:, :].rearrange("p (c n) -> p c n", n=P),
                                per_chunk(cw1, 4 * g, 4 * g + 4, P), ALU.mult).then_inc(s_z, 1)
                V.tensor_tensor(seg[:, g * HALF:(g + 1) * HALF].rearrange("p (c n) -> p c n", n=P),
                                ps_t[g][:, :].rearrange("p (c n) -> p c n", n=P),
                                per_chunk(cw0, 4 * g, 4 * g + 4, P), ALU.mult).then_inc(s_z2, 1)

            def mask(i, g):
                dve.wait_ge(s_sp, 4 * i + g + 1)
                after(dve, s_op, 4 * i + g - 1)
                if g < 2:
                    dve.wait_ge(s_ktp, i + 1)
                V.tensor_tensor(probs[g % 2].rearrange("p (h l) -> p h l", h=HG),
                                ps_s[g % 2][:, :].rearrange("p (h l) -> p h l", h=HG),
                                causal_m[:, :].rearrange("p (o l) -> p o l", o=1)
                                .to_broadcast([P, HG, P]), ALU.mult).then_inc(s_p, 1)

            def gate_scale(i):
                dve.wait_ge(s_sg, 2 * (i + 1))
                after(dve, s_us, i)
                V.tensor_reduce(gmx, sg, AX_X, ALU.max, apply_absolute_value=True).then_inc(s_gm, 1)
                dve.wait_ge(s_gm, i + 1)
                V.tensor_scalar(gmx, gmx, TINY, None, ALU.max).then_inc(s_gm2, 1)
                dve.wait_ge(s_gm2, i + 1)
                after(dve, s_gs, i)
                V.reciprocal(grc, gmx).then_inc(s_rg, 1)
                after(dve, s_fin, 2 * i)
                V.tensor_scalar(usc, base, gmx, HEAD_BOUND / G_TOP, ALU.mult, ALU.mult).then_inc(s_us, 1)
                dve.wait_ge(s_rg, i + 1)
                V.tensor_scalar(gsc, grc, G_TOP / HEAD_BOUND, None, ALU.mult).then_inc(s_gs, 1)

            def first_norm(j, slot):
                dve.wait_ge(s_x, 16 * (j + 1))
                norm_stats(j, x_ring[:, slot, :], st1, mv1, s_bn1, s_ag1)

            def q_block(i, g):
                dve.wait_ge(s_qt, i + 1)
                after(dve, s_sp, 4 * i + g - 1)
                if g < 2:
                    after(dve, s_up, 2 * i)
                V.tensor_tensor(q_blk[g % 2].rearrange("p (h l) -> p h l", h=HG),
                                q_sb[:, g * P:(g + 1) * P].rearrange("p (o l) -> p o l", o=1)
                                .to_broadcast([P, HG, P]),
                                head_m[:, :].rearrange("p (h o) -> p h o", o=1).to_broadcast([P, HG, P]),
                                ALU.mult).then_inc(s_qb, 1)

            def head_out(i, g):
                dve.wait_ge(s_op, 4 * i + g + 1)
                after(dve, s_gtp, 2 * i)
                both = ps_o[g % 2][:, :].rearrange("p (h s d) -> p h s d", h=HG, s=2)
                part = by_head(tmp[:, g * HG * DV:(g + 1) * HG * DV], DV)
                V.tensor_tensor(part, both[:, :, 1, :], per_head(sgn, g * HG, (g + 1) * HG, DV), ALU.mult)\
                 .then_inc(s_ob, 1)
                dve.wait_ge(s_ob, 5 * i + g + 2)
                V.tensor_tensor(by_head(o_sb[:, g * HG * DV:(g + 1) * HG * DV], DV), both[:, :, 0, :], part,
                                ALU.add).then_inc(s_o, 1)

            pipeline(dve, step)

        @block.gpsimd
        def _(pool):
            G = nc.gpsimd
            U = len(UNITS)
            for n, u in enumerate([U] + list(range(U))):
                pool.wait_ge(s_wmax, n + 1)
                G.partition_all_reduce(mx[:, u:u + 1], mx[:, u:u + 1], P, AMAX).then_inc(s_wall, 1)
            pool.wait_ge(s_cv, 14)

            def norm_scale(j, mv, ve, rs, nm, nb, shift, s_ag, s_rs, s_nb):
                pool.wait_ge(s_ag, j + 1)
                G.tensor_tensor(ve, mv[:, 1:2], eps_c[:, 0:1], ALU.add).then_inc(s_rs, 1)
                pool.wait_ge(s_rs, 3 * j + 1)
                G.tensor_tensor(rs, ve, nhalf[:, 0:1], ALU.pow).then_inc(s_rs, 1)
                pool.wait_ge(s_rs, 3 * j + 2)
                after(pool, s_nb, j)
                G.tensor_tensor(nm, mv[:, 0:1], rs, ALU.mult).then_inc(s_rs, 1)
                pool.wait_ge(s_rs, 3 * j + 3)
                G.tensor_tensor(nb, shift, nm, ALU.subtract).then_inc(s_nb, 1)

            def exp_kv(j):
                pool.wait_ge(s_e, j + 1)
                pool.wait_ge(s_vl, 16 * (j + 1))
                G.tensor_tensor(vx[:, :], vx[:, :], ek[:, :], ALU.mult).then_inc(s_ev, 1)

            def head_factors(p):
                pool.wait_ge(s_ss, p + 1)
                pool.wait_ge(s_cf, p + 1)
                G.tensor_tensor(ftmp, coef, coef, ALU.mult).then_inc(s_fp, 1)
                pool.wait_ge(s_fp, 6 * p + 1)
                G.tensor_tensor(ftmp, ftmp, ossq, ALU.mult).then_inc(s_fp, 1)
                pool.wait_ge(s_fp, 6 * p + 2)
                G.tensor_tensor(ftmp, ftmp, dv_c, ALU.mult).then_inc(s_fp, 1)
                pool.wait_ge(s_fp, 6 * p + 3)
                G.tensor_tensor(ftmp, ftmp, eps_c, ALU.add).then_inc(s_fp, 1)
                pool.wait_ge(s_fp, 6 * p + 4)
                G.tensor_tensor(fac, ftmp, nhalf, ALU.pow).then_inc(s_fp, 1)
                pool.wait_ge(s_fp, 6 * p + 5)
                G.tensor_tensor(fac, fac, coef, ALU.mult).then_inc(s_fp, 1)
                pool.wait_ge(s_fp, 6 * p + 6)
                pool.wait_ge(s_gs, p + 1)
                G.tensor_tensor(fac, fac, gsc.to_broadcast([P, H]), ALU.mult).then_inc(s_f, 1)

            def step(i, slot, main, nxt, nxt2, prev):
                n, p = i + 1, i - 1
                if prev:
                    pool.wait_ge(s_sq, p + 1)
                    pool.wait_ge(s_sg, 2 * (p + 1))
                    G.tensor_tensor(o_sb, o_sb, sg, ALU.mult).then_inc(s_og, 1)
                if prev:
                    head_factors(p)
                if main:
                    pool.wait_ge(s_k, i + 1)
                    after(pool, s_op, 4 * i)
                    after(pool, s_o, 4 * i)
                    rotate(pool, G, i, 1, k_sb, rot_k, s_r1k, s_rk)
                    pool.wait_ge(s_rk, i + 1)
                    pool.wait_ge(s_rq, i + 1)
                    for g in range(2):
                        pool.wait_ge(s_vc, 2 * i + g + 1)
                        G.tensor_tensor(by_head(tmp[:, g * HALF:(g + 1) * HALF], DV), v2[:, g * 8:(g + 1) * 8, 0, :],
                                        by_head(router_d[:, g * HALF:(g + 1) * HALF], DV), ALU.mult)\
                         .then_inc(s_vr, 1)
                if nxt:
                    norm_scale(n, mv2, ve2, rs2, nm2, nb2, shift2, s_ag2, s_rs2, s_nb2)
                if main:
                    pool.wait_ge(s_sgn, i + 1)
                    G.tensor_tensor(v2[:, :, 1, :], v2[:, :, 0, :], per_head(sgn, 0, H, DV), ALU.mult)\
                     .then_inc(s_sv, 1)
                if nxt2:
                    norm_scale(i + 2, mv1, ve1, rs1, nm1, nb1, shift1, s_ag1, s_rs1, s_nb1)
                if nxt2:
                    exp_kv(i + 2)

            pipeline(pool, step)


_INPUTS = ("x", "ctx_2048", "g_xattn", "g_ffn", "decay", "first", "conv", "wq", "wk", "wv", "wg", "router", "wout",
           "identity", "causal", "cos", "sin", "count", "heads")


def _shape_constants():
    import numpy as np

    f = np.float32
    t, b = np.arange(P) // NB, np.arange(P) % NB
    inv_freq = (f(1.0) / f(10000.0) ** (np.arange(0, DK, 2, dtype=f) / f(DK))).astype(f)
    angle = b.astype(f)[:, None] * inv_freq[None, :]
    cos, sin = np.cos(angle).astype(f), np.sin(angle).astype(f)
    return {
        "identity": np.eye(P, dtype=f),
        "causal": ((t[:, None] == t[None, :]) & (b[:, None] <= b[None, :])).astype(f),
        "cos": np.concatenate([cos, cos], axis=1),
        "sin": np.concatenate([-sin, sin], axis=1),
        "count": (b + 1).astype(f)[:, None],
        "heads": (np.arange(P)[:, None] // DK == np.arange(HG)[None, :]).astype(f),
    }


def kernel(**inputs):
    import numpy as np
    import concourse.bacc as bacc
    from concourse.bass_utils import run_bass_kernel_spmd

    a = {n: np.asarray(v) for n, v in inputs.items()}
    layout = {
        "x": a["x"], "ctx_2048": a["ctx_2048"],
        "g_xattn": a["g_xattn"].reshape(1, 1), "g_ffn": a["g_ffn"].reshape(1, 1),
        "decay": a["L0_xattn_time_decay"].reshape(KC, P).T, "first": a["L0_xattn_time_first"].reshape(KC, P).T,
        "conv": a["L0_ffn_conv_w"].reshape(KC, P, 2).transpose(2, 1, 0),
        "wq": a["L0_ffn_Wq"], "wk": a["L0_ffn_Wk"], "wv": a["L0_ffn_Wv"], "wg": a["L0_ffn_Wg"],
        "router": a["L0_ffn_router_w"].reshape(C, 2).T, "wout": a["L0_ffn_Wout"],
        **_shape_constants(),
    }
    nc = bacc.Bacc("TRN2", target_bir_lowering=False, num_devices=1)
    arrays, args = {}, []
    for name in _INPUTS:
        arr = np.ascontiguousarray(layout[name])
        arrays[f"in_{name}"] = arr
        args.append(nc.dram_tensor(f"in_{name}", arr.shape, mybir.dt.from_np(arr.dtype), kind="ExternalInput").ap())
    out = nc.dram_tensor("out", a["x"].shape, F32, kind="ExternalOutput").ap()
    flamingo_layer(nc, *args, out)
    r = run_bass_kernel_spmd(nc, [arrays], core_ids=[0])
    return r.results[0]["out"]
```

```python
from contextlib import ExitStack

import concourse.bass as bass
from concourse import mybir

F32 = mybir.dt.float32
F16 = mybir.dt.float16
BF16 = mybir.dt.bfloat16
ALU = mybir.AluOpType
ACT = mybir.ActivationFunctionType
AX_X = mybir.AxisListType.X
AMAX = bass.bass_isa.ReduceOp.max

P = 128
NB = 8
TT = P // NB
SEG = TT + 1
C = 1024
KC = C // P
HALF = C // 2
H = 16
DK = 32
DV = 64
HG = 4
NG = H // HG
EPS = 1e-5
SHIFT = 40.0
U_MAX = 87.0
TINY = 1e-30
LN_BOUND = float(C) ** 0.5
HEAD_BOUND = float(DV) ** 0.5
W_TOP = 2.0 ** 14
H_TOP = 2.0 ** 15
G_TOP = 2.0 ** 14
UNITS = ("q", "k", "v0", "v1", "g0", "g1", "o0", "o1")
UQ, UK, UV, UG, UO = 0, 1, 2, 4, 6


def flamingo_layer(nc, x, ctxt, g_xattn, g_ffn, decay_cols, first_cols, conv_cols, w_q, w_k, w_v, w_g,
                   router, w_out, identity, causal, cos_rows, sin_rows, count_rows, head_rows, out):
    T = x.shape[1]
    N = T // TT
    LOOPED = (N - 3) // 3 * 3
    x_t = x.rearrange("b t c -> t b c")
    v_t = ctxt.rearrange("b t c -> t b c")
    out_t = out.rearrange("b t c -> t b c")
    w_src = [w_q, w_k, w_v[:, 0:HALF], w_v[:, HALF:C], w_g[:, 0:HALF], w_g[:, HALF:C],
             w_out[:, 0:HALF], w_out[:, HALF:C]]

    with ExitStack() as ctx:
        def sb(name, shape, dt=F32):
            return ctx.enter_context(nc.sbuf_tensor(name, shape, dt))

        def bank(name):
            return ctx.enter_context(nc.psum_tensor(name, [P, HALF], F32))

        def sem(name):
            return ctx.enter_context(nc.semaphore(name))

        w_hi = sb("w_hi", [P, len(UNITS), KC, HALF], F16)
        w_lo = sb("w_lo", [P, len(UNITS), KC, HALF], F16)
        x_ring = sb("x_ring", [P, 3, C])
        vx = sb("vx", [P, C])
        ek = sb("ek", [P, C])
        decay = sb("decay", [P, KC * NB * SEG])
        seg = sb("seg", [P, KC * NB * SEG])
        fa = sb("fa", [P, C])
        fb = sb("fb", [P, C])
        h_hi = sb("h_hi", [P, C], F16)
        h_lo = sb("h_lo", [P, C], F16)
        work = sb("work", [P, 2, KC * HALF])
        v2 = work[:, 0, 0:2 * C].rearrange("p (h s d) -> p h s d", h=H, s=2)
        sg = work[:, 0, 2 * C:3 * C]
        o_sb = work[:, 0, 3 * C:4 * C]
        q_sb = work[:, 1, 0:HALF]
        k_sb = work[:, 1, HALF:C]
        rot_q = work[:, 1, C:C + HALF]
        rot_k = work[:, 1, C + HALF:2 * C]
        probs = (rot_q, rot_k)
        g_split = work[:, 1, 2 * C:3 * C].bitcast(F16)
        gt_hi, gt_lo = g_split[:, 0:C], g_split[:, C:2 * C]
        q_blk = (work[:, 1, 2 * C:2 * C + HALF], work[:, 1, 2 * C + HALF:3 * C])
        squares = work[:, 1, 2 * C:3 * C]
        tmp = work[:, 1, 3 * C:4 * C]
        router_d = sb("router_d", [P, C])
        ident = sb("ident", [P, P])
        causal_m = sb("causal_m", [P, P])
        cos2 = sb("cos2", [P, DK])
        sin2 = sb("sin2", [P, DK])
        cnt_c = sb("cnt_c", [P, 1])
        head_m = sb("head_m", [P, HG])
        small = sb("small", [P, 360])
        at = [0]

        def col(n):
            at[0] += n
            return small[:, at[0] - n:at[0]]

        dk = col(KC)
        eu = col(KC)
        cw0, cw1 = col(KC), col(KC)
        mx = col(len(UNITS) + 1)
        sw = col(len(UNITS) + 1)
        inv = col(len(UNITS))
        tg = col(2)
        base = col(2)
        nhalf = col(H)
        eps_c, dv_c = col(H), col(H)
        shift1, shift2 = col(1), col(1)
        st1, st2 = col(12), col(12)
        mv1, mv2 = col(2), col(2)
        ve1, ve2 = col(1), col(1)
        rs1, rs2 = col(1), col(1)
        nm1, nm2 = col(1), col(1)
        nb1, nb2 = col(1), col(1)
        delta = col(H)
        sgn = col(H)
        pr = col(H)
        coef = col(H)
        ctmp = col(H)
        osum = col(H)
        ossq = col(H)
        ftmp = col(H)
        fac = col(H)
        gmx = col(1)
        grc = col(1)
        gsc = col(1)
        usc = col(2)
        carry_b = sb("carry_b", [P, KC * NB])
        carry_a = sb("carry_a", [P, KC * NB])

        ps_t = (bank("ps_t0"), bank("ps_t1"))
        ps_g = (bank("ps_g0"), bank("ps_g1"))
        ps_s = (bank("ps_s0"), bank("ps_s1"))
        ps_o = (bank("ps_o0"), bank("ps_o1"))

        s_const, s_w = sem("const_loaded"), [sem(f"weight_loaded{n}") for n in range(4)]
        s_x, s_vl, s_store = sem("x_loaded"), sem("v_loaded"), sem("out_stored")
        s_cwmax, s_wsum, s_wall, s_wsc, s_whi, s_wlo = (sem(n) for n in
            ("conv_bound", "wsum_done", "wbound_all", "wscale_done", "whi_done", "wlo_done"))
        s_router, s_base = sem("router_loaded"), sem("base_done")
        s_ca, s_cv, s_cp = sem("const_act"), sem("const_dve"), sem("const_pool")
        s_etp, s_evp, s_yp, s_xnp = sem("ek_transposed"), sem("ev_transposed"), sem("y_transposed"), sem("xn_transposed")
        s_qp, s_kp, s_vp, s_gp, s_up = sem("q_proj"), sem("k_proj"), sem("v_proj"), sem("g_proj"), sem("out_proj")
        s_qtp, s_ktp, s_gtp = sem("q_transposed"), sem("k_transposed"), sem("gated_transposed")
        s_cump, s_sp, s_op = sem("cum_matmul"), sem("scores_matmul"), sem("o_matmul")
        s_bn1, s_ag1, s_rs1, s_nb1, s_e, s_ev = (sem(n) for n in
            ("bn1", "aggr1", "rstd1", "nbias1", "ek_done", "ev_done"))
        s_sega, s_segb = sem("seg_den_copied"), sem("seg_num_copied")
        s_fda, s_fdb = sem("first_den"), sem("first_num")
        s_sca, s_scb, s_sva, s_svb = sem("scan_den"), sem("scan_num"), sem("save_den"), sem("save_num")
        s_den, s_num, s_rec, s_y, s_x2 = (sem(n) for n in
            ("den_done", "num_done", "recip_done", "y_done", "x2_done"))
        s_bn2, s_ag2, s_rs2, s_nb2, s_xn = (sem(n) for n in
            ("bn2", "aggr2", "rstd2", "nbias2", "xn_done"))
        s_z, s_z2, s_pre, s_h, s_hhi, s_hlo = (sem(n) for n in
            ("conv_now", "conv_past", "conv_done", "h_done", "h_hi_done", "h_lo_done"))
        s_q, s_k, s_vc = sem("q_copied"), sem("k_copied"), sem("v_copied")
        s_r1q, s_r1k, s_rq, s_rk = sem("rot_q_part"), sem("rot_k_part"), sem("rot_q"), sem("rot_k")
        s_qt, s_kt = sem("qt_copied"), sem("kt_copied")
        s_vr, s_dl = sem("v_router"), sem("delta_done")
        s_sgn, s_sv, s_th, s_pr, s_cum, s_cf = (sem(n) for n in
            ("sign_done", "signed_v", "tanh_done", "prob_done", "cum_done", "coef_done"))
        s_sm = sem("dve_small")
        s_qb, s_p, s_ob, s_o = sem("q_block"), sem("probs_done"), sem("o_part"), sem("o_done")
        s_os, s_oc, s_sq, s_ss = sem("o_sum"), sem("o_centred"), sem("o_square"), sem("o_var")
        s_os2 = sem("o_mean")
        s_fp, s_f, s_og, s_gt = sem("factor_part"), sem("factor"), sem("o_times_gate"), sem("gated")
        s_gthi, s_gtlo = sem("gt_hi"), sem("gt_lo")
        s_sg, s_gm, s_gm2, s_gs, s_us = (sem(n) for n in
            ("silu_g", "gate_max", "gate_max_guard", "gate_scale", "out_scale"))
        s_fin = sem("final_done")
        s_rg, s_y0 = sem("gate_recip"), sem("first_step_state")

        block = ctx.enter_context(nc.Block())

        flat = "p u k n -> p (u k n)"
        stage = (w_hi[:, UO:UO + 2, :, :].rearrange(flat).bitcast(F32),
                 w_lo[:, UO:UO + 2, :, :].rearrange(flat).bitcast(F32), work[:, 0, :], work[:, 1, :])

        def wait_lo(eng, u):
            eng.wait_ge(s_wlo, u + 1)

        def unit(w, u):
            return w[:, u, :, :].rearrange("p k n -> p (k n)")

        def seg4(lo, hi):
            return seg[:, :].rearrange("p (c b t) -> p c t b", c=KC, b=NB)[:, :, lo:hi, :]

        seg_rows = seg[:, :].rearrange("p (s t) -> p s t", t=SEG)

        def tok(ap):
            return ap.rearrange("p (c t b) -> p c t b", t=TT, b=NB)

        def per_chunk(cols, lo, hi, n):
            return cols[:, lo:hi].rearrange("p (c o) -> p c o", o=1).to_broadcast([P, hi - lo, n])

        def per_head(cols, lo, hi, n):
            return cols[:, lo:hi].rearrange("p (h o) -> p h o", o=1).to_broadcast([P, hi - lo, n])

        def by_head(ap, d):
            return ap.rearrange("p (h d) -> p h d", d=d)

        def after(eng, s, value):
            if not isinstance(value, int) or value > 0:
                eng.wait_ge(s, value)

        def pipeline(eng, step):
            step(0, 0, True, True, True, False)
            with eng.Fori(1, LOOPED + 1, 3) as i:
                for r in range(3):
                    step(i + r, (1 + r) % 3, True, True, True, True)
            for i in range(LOOPED + 1, N - 2):
                step(i, i % 3, True, True, True, True)
            step(N - 2, (N - 2) % 3, True, True, False, True)
            step(N - 1, (N - 1) % 3, True, False, False, True)
            step(N, N % 3, False, False, False, True)

        def rotate(eng, E, i, half_of_tmp, src, dst, parts, done):
            scratch = tmp[:, half_of_tmp * HALF:(half_of_tmp + 1) * HALF]
            s4 = src.rearrange("p (h s d) -> p h s d", h=H, s=2)
            t4 = scratch.rearrange("p (h s d) -> p h s d", h=H, s=2)
            half = DK // 2
            E.tensor_tensor(by_head(dst, DK), by_head(src, DK),
                            cos2[:, :].rearrange("p (o d) -> p o d", o=1).to_broadcast([P, H, DK]), ALU.mult)\
             .then_inc(parts, 1)
            for s in range(2):
                E.tensor_tensor(t4[:, :, s, :], s4[:, :, 1 - s, :],
                                sin2[:, s * half:(s + 1) * half].rearrange("p (o d) -> p o d", o=1)
                                .to_broadcast([P, H, half]), ALU.mult).then_inc(parts, 1)
            eng.wait_ge(parts, 3 * (i + 1))
            E.tensor_tensor(dst, dst, scratch, ALU.add).then_inc(done, 1)

        @block.sync
        def _(sp):
            def load_x(j, slot):
                sp.dma_start(x_ring[:, slot, :], x_t[bass.ds(j * TT, TT), :, :]).then_inc(s_x, 16)

            def load_v(j):
                sp.dma_start(vx[:, :], v_t[bass.ds(j * TT, TT), :, :]).then_inc(s_vl, 16)

            def load_unit(u):
                if u >= 4:
                    sp.wait_ge(s_whi, u - 3)
                    wait_lo(sp, u - 4)
                sp.dma_start(stage[u % 4].rearrange("p (k n) -> p k n", k=KC),
                             w_src[u].rearrange("(k p) n -> p k n", p=P)).then_inc(s_w[u % 4], 16)

            load_x(0, 0)
            load_v(0)
            for dst, src in ((dk, decay_cols), (eu, first_cols), (cw0, conv_cols[0]), (cw1, conv_cols[1]),
                             (ident[:, :], identity), (tg[:, 0:1], g_xattn.to_broadcast([P, 1])),
                             (tg[:, 1:2], g_ffn.to_broadcast([P, 1]))):
                sp.dma_start(dst, src).then_inc(s_const, 16)
            load_unit(0)
            load_unit(1)
            load_x(1, 1)
            load_unit(2)
            load_unit(3)
            for dst, src in ((causal_m[:, :], causal), (cos2[:, :], cos_rows), (sin2[:, :], sin_rows),
                             (cnt_c[:, :], count_rows), (head_m[:, :], head_rows),
                             (router_d[:, :], router[0:1, :].to_broadcast([P, C])),
                             (x_ring[:, 2, :], router[1:2, :].to_broadcast([P, C]))):
                sp.dma_start(dst, src).then_inc(s_router, 16)
            load_unit(4)
            load_unit(5)
            sp.wait_ge(s_xnp, 2)
            load_v(1)
            load_unit(6)
            load_unit(7)
            sp.wait_ge(s_base, 1)

            def step(i, slot, main, nxt, nxt2, prev):
                if prev:
                    after(sp, s_fin, 2 * i)
                    sp.dma_start(out_t[bass.ds((i - 1) * TT, TT), :, :], x_ring[:, (slot + 2) % 3, :])\
                      .then_inc(s_store, 16)
                if nxt2:
                    after(sp, s_store, 16 * i)
                    load_x(i + 2, (slot + 2) % 3)
                    after(sp, s_xnp, 2 * (i + 2))
                    load_v(i + 2)

            pipeline(sp, step)
            sp.wait_ge(s_store, 16 * N)

        @block.tensor
        def _(pe):
            def transposes(dst, src, s):
                for n in range(4):
                    last = nc.tensor.transpose(dst[:, n * P:(n + 1) * P], src[:, n * P:(n + 1) * P], ident[:, :])
                last.then_inc(s, 1)

            def project(dst, a_hi, a_lo, u, s, part=None):
                for kc in range(KC) if part is None else range(part * KC // 2, (part + 1) * KC // 2):
                    hi, lo = (a[:, kc * P:(kc + 1) * P] for a in (a_hi, a_lo))
                    nc.tensor.matmul(dst[:, :], hi, w_hi[:, u, kc, :], start=(kc == 0), stop=False)
                    nc.tensor.matmul(dst[:, :], hi, w_lo[:, u, kc, :], start=False, stop=False)
                    last = nc.tensor.matmul(dst[:, :], lo, w_hi[:, u, kc, :], start=False, stop=(kc == KC - 1))
                if part != 0:
                    last.then_inc(s, 1)

            def unit_ready(i, u):
                if isinstance(i, int) and i == 0:
                    pe.wait_ge(s_whi, u + 1)
                    wait_lo(pe, u)

            def step(i, slot, main, nxt, nxt2, prev):
                n, p = i + 1, i - 1
                if main:
                    unit_ready(i, UQ)
                    after(pe, s_hlo, 2 * i + 1)
                    after(pe, s_sg, 2 * i - 1)
                    project(ps_g[0], h_hi, h_lo, UQ, s_qp, 0)
                if nxt:
                    for g in range(2):
                        after(pe, s_e, n + 1)
                        after(pe, s_z, 2 * n)
                        after(pe, s_z2, 2 * n)
                        transposes(ps_t[g], ek[:, g * HALF:(g + 1) * HALF], s_etp)
                if main:
                    after(pe, s_hlo, 2 * (i + 1))
                    project(ps_g[0], h_hi, h_lo, UQ, s_qp, 1)
                    unit_ready(i, UK)
                    after(pe, s_sg, 2 * i)
                    project(ps_g[1], h_hi, h_lo, UK, s_kp, 0)
                if nxt:
                    for g in range(2):
                        after(pe, s_ev, n + 1)
                        after(pe, s_fda, 2 * n + g + 1)
                        transposes(ps_t[g], vx[:, g * HALF:(g + 1) * HALF], s_evp)
                if main:
                    project(ps_g[1], h_hi, h_lo, UK, s_kp, 1)
                    unit_ready(i, UV)
                    after(pe, s_q, i + 1)
                    project(ps_g[0], h_hi, h_lo, UV, s_vp)
                    for g in range(2):
                        after(pe, (s_rq, s_rk)[g], i + 1)
                        if nxt:
                            after(pe, s_fdb, 2 * n + g + 1)
                        elif g == 0:
                            after(pe, s_z, 2 * (i + 1))
                            after(pe, s_z2, 2 * (i + 1))
                        transposes(ps_t[g], (rot_q, rot_k)[g], (s_qtp, s_ktp)[g])
                    unit_ready(i, UV + 1)
                    after(pe, s_k, i + 1)
                    project(ps_g[1], h_hi, h_lo, UV + 1, s_vp, 0)
                if prev:
                    for g in range(2):
                        after(pe, s_gt, p + 1)
                        if main:
                            after(pe, (s_qt, s_kt)[g], i + 1)
                        else:
                            after(pe, s_gtlo, 2 * p)
                        transposes(ps_t[g], o_sb[:, g * HALF:(g + 1) * HALF], s_gtp)
                if main:
                    project(ps_g[1], h_hi, h_lo, UV + 1, s_vp, 1)
                if prev:
                    for g in range(2):
                        if main:
                            after(pe, s_vc, 2 * i + g + 1)
                        else:
                            after(pe, s_sg, 2 * p + g + 1)
                        for part in range(2):
                            if g == 0:
                                after(pe, s_gtlo, 2 * p + part + 1)
                            project(ps_g[g], gt_hi, gt_lo, UO + g, s_up, part)
                            if nxt and (g, part) == (0, 1):
                                y_transposes(n, p, prev)
                elif nxt:
                    y_transposes(n, p, prev)
                if main:
                    after(pe, s_sgn, i + 1)
                    after(pe, s_p, 4 * i)
                    nc.tensor.matmul(ps_s[0][:, 0:H], causal_m[:, :], sgn, start=True, stop=True)\
                      .then_inc(s_cump, 1)
                if nxt:
                    for g in range(2):
                        after(pe, s_xn, n + 1)
                        after(pe, s_x2, 2 * n + g + 1)
                        transposes(ps_t[g], vx[:, g * HALF:(g + 1) * HALF], s_xnp)
                if main:
                    for g in range(2):
                        unit_ready(i, UG + g)
                        if prev:
                            after(pe, s_fin, 2 * p + g + 1)
                        else:
                            after(pe, s_vc, 2 * i + g + 1)
                        for part in range(2):
                            project(ps_g[g], h_hi, h_lo, UG + g, s_gp, part)
                            if (g, part) == (0, 0):
                                scores(i, 0)
                                scores(i, 1)
                            elif (g, part) != (1, 1):
                                values(i, g)
                                scores(i, g + 2)
                    values(i, 2)
                    values(i, 3)

            def y_transposes(n, p, prev):
                for g in range(2):
                    after(pe, s_y, 2 * n + g + 1)
                    after(pe, s_fdb, 2 * n + g + 1)
                    if prev:
                        after(pe, s_gtlo, 2 * p + g + 1)
                    elif not isinstance(n, int) or n >= 1:
                        after(pe, (s_qt, s_kt)[g], n)
                    transposes(ps_t[g], fb[:, g * HALF:(g + 1) * HALF], s_yp)

            def scores(i, g):
                after(pe, s_qb, 4 * i + g + 1)
                after(pe, s_kt, i + 1)
                after(pe, s_p, 4 * i + g - 1)
                if g == 0:
                    after(pe, s_cum, i + 1)
                nc.tensor.matmul(ps_s[g % 2][:, :], k_sb[:, g * P:(g + 1) * P], q_blk[g % 2],
                                 start=True, stop=True).then_inc(s_sp, 1)

            def values(i, g):
                after(pe, s_p, 4 * i + g + 1)
                after(pe, s_sv, i + 1)
                after(pe, s_o, 4 * i + g - 1)
                for h in range(HG):
                    last = nc.tensor.matmul(ps_o[g % 2][:, h * P:(h + 1) * P], probs[g % 2][:, h * P:(h + 1) * P],
                                            v2[:, g * HG + h, :, :].rearrange("p s d -> p (s d)"),
                                            start=True, stop=True)
                last.then_inc(s_op, 1)

            pe.wait_ge(s_const, 16 * 7)
            step(-1, 2, False, True, True, False)
            pipeline(pe, step)

        @block.scalar
        def _(act):
            A = nc.scalar.activation
            act.wait_ge(s_const, 16 * 7)
            A(dk, dk, ACT.Exp).then_inc(s_ca, 1)
            act.wait_ge(s_ca, 1)
            A(dk, dk, ACT.Exp, scale=-1.0).then_inc(s_ca, 1)
            act.wait_ge(s_cv, 9)
            A(eu, eu, ACT.Exp).then_inc(s_ca, 1)
            A(tg, tg, ACT.Tanh).then_inc(s_ca, 1)
            A(delta[:, 0:KC], cw0, ACT.Abs).then_inc(s_ca, 1)
            A(sgn[:, 0:KC], cw1, ACT.Abs).then_inc(s_ca, 1)

            def bound_unit(u):
                act.wait_ge(s_w[u % 4], 16 * (u // 4 + 1))
                if u >= UO:
                    wait_lo(act, UG)
                A(unit(w_hi, u).bitcast(BF16), stage[u % 4], ACT.Abs, accum_out=mx[:, u:u + 1]).then_inc(s_wsum, 1)

            def split_unit(u):
                act.wait_ge(s_wsc, u + 1)
                A(unit(w_hi, u), stage[u % 4], ACT.Copy, scale=sw[:, u:u + 1]).then_inc(s_whi, 1)

            def exp_k(j, slot):
                act.wait_ge(s_nb1, j + 1)
                after(act, s_etp, 2 * j)
                A(ek[:, :], x_ring[:, slot, :], ACT.Exp, scale=rs1, bias=nb1).then_inc(s_e, 1)

            def fill_segments(j, ps_sem, carry, saved, free, free_at, done):
                after(act, free, free_at)
                after(act, saved, j)
                A(seg_rows[:, :, 0], carry[:, :], ACT.Copy).then_inc(done, 1)
                for g in range(2):
                    act.wait_ge(ps_sem, 2 * j + g + 1)
                    A(seg4(1, SEG)[:, g * 4:(g + 1) * 4, :, :], tok(ps_t[g][:, :]), ACT.Copy).then_inc(done, 1)

            def step(i, slot, main, nxt, nxt2, prev):
                n, p = i + 1, i - 1
                if nxt:
                    fill_denominator(n)
                if prev:
                    after(act, s_oc, p + 1)
                    after(act, s_sp, 4 * (p + 1))
                    A(squares, o_sb, ACT.Square).then_inc(s_sq, 1)
                if main:
                    if isinstance(i, int) and i == 0:
                        wait_lo(act, UO)
                        wait_lo(act, UO + 1)
                    act.wait_ge(s_qp, i + 1)
                    after(act, s_qb, 4 * i)
                    A(q_sb, ps_g[0][:, :], ACT.Silu, scale=inv[:, UQ:UQ + 1]).then_inc(s_q, 1)
                    if nxt:
                        fill_numerator(n)
                    act.wait_ge(s_kp, i + 1)
                    after(act, s_sp, 4 * i)
                    A(k_sb, ps_g[1][:, :], ACT.Copy, scale=inv[:, UK:UK + 1]).then_inc(s_k, 1)
                elif nxt:
                    fill_numerator(n)
                if main:
                    copy_v(i, 0)
                    act.wait_ge(s_qtp, i + 1)
                    A(q_sb, ps_t[0][:, :], ACT.Copy).then_inc(s_qt, 1)
                    act.wait_ge(s_ktp, i + 1)
                    A(k_sb, ps_t[1][:, :], ACT.Copy).then_inc(s_kt, 1)
                if prev:
                    for g in range(2):
                        act.wait_ge(s_gtp, 2 * p + g + 1)
                        act.wait_ge(s_ss, p + 1)
                        A(gt_hi[:, g * HALF:(g + 1) * HALF], ps_t[g][:, :], ACT.Copy).then_inc(s_gthi, 1)
                if main:
                    copy_v(i, 1)
                    act.wait_ge(s_dl, 2 * (i + 1))
                    after(act, s_cf, i)
                    A(pr, delta, ACT.Abs).then_inc(s_th, 1)
                    act.wait_ge(s_th, 2 * i + 1)
                    A(pr, pr, ACT.Tanh, scale=0.5).then_inc(s_th, 1)
                if nxt:
                    normed_x(n, (slot + 1) % 3)
                if main:
                    silu_gate(i, 0)
                if nxt:
                    silu_h(n)
                    split_h(n, 0)
                if main:
                    silu_gate(i, 1)
                if nxt:
                    split_h(n, 1)
                if nxt2:
                    exp_k(i + 2, (slot + 2) % 3)

            def fill_denominator(n):
                fill_segments(n, s_etp, carry_b, s_sva, s_pre, n, s_sega)

            def normed_x(n, slot):
                act.wait_ge(s_nb2, n + 1)
                act.wait_ge(s_evp, 2 * n + 2)
                A(vx[:, :], x_ring[:, slot, :], ACT.Identity, scale=rs2, bias=nb2).then_inc(s_xn, 1)

            def silu_h(n):
                act.wait_ge(s_pre, n + 1)
                A(fa[:, :], fa[:, :], ACT.Silu).then_inc(s_h, 1)

            def split_h(n, g):
                act.wait_ge(s_h, n + 1)
                after(act, s_gp, 2 * n)
                A(h_hi[:, g * HALF:(g + 1) * HALF], fa[:, g * HALF:(g + 1) * HALF], ACT.Copy,
                  scale=sw[:, len(UNITS):len(UNITS) + 1]).then_inc(s_hhi, 1)

            def fill_numerator(n):
                act.wait_ge(s_sva, n + 1)
                fill_segments(n, s_evp, carry_a, s_svb, s_den, n + 1, s_segb)

            def silu_gate(i, g):
                act.wait_ge(s_gp, 2 * i + g + 1)
                after(act, s_og, i)
                after(act, s_gm, i)
                A(sg[:, g * HALF:(g + 1) * HALF], ps_g[g][:, :], ACT.Silu,
                  scale=inv[:, UG + g:UG + g + 1]).then_inc(s_sg, 1)

            def copy_v(i, g):
                act.wait_ge(s_vp, 2 * i + g + 1)
                after(act, s_op, 4 * i)
                A(v2[:, g * 8:(g + 1) * 8, 0, :], by_head(ps_g[g][:, :], DV), ACT.Copy,
                  scale=inv[:, UV + g:UV + g + 1]).then_inc(s_vc, 1)

            exp_k(0, 0)
            fill_denominator(0)
            bound_unit(0)
            fill_numerator(0)
            bound_unit(1)
            split_unit(0)
            bound_unit(2)
            split_unit(1)
            bound_unit(3)
            split_unit(2)
            normed_x(0, 0)
            bound_unit(4)
            split_unit(3)
            silu_h(0)
            split_h(0, 0)
            split_h(0, 1)
            split_unit(4)
            bound_unit(5)
            split_unit(5)
            exp_k(1, 1)
            bound_unit(6)
            split_unit(6)
            bound_unit(7)
            split_unit(7)
            pipeline(act, step)

        @block.vector
        def _(dve):
            V = nc.vector
            U = len(UNITS)

            def scale_of(u, top, count):
                dve.wait_ge(s_wall, count)
                V.tensor_scalar(mx[:, u:u + 1], mx[:, u:u + 1], TINY, None, ALU.max).then_inc(s_sm, 1)
                dve.wait_ge(s_sm, 3 * count - 2)
                V.reciprocal(sw[:, u:u + 1], mx[:, u:u + 1]).then_inc(s_sm, 1)
                dve.wait_ge(s_sm, 3 * count - 1)
                V.tensor_scalar(sw[:, u:u + 1], sw[:, u:u + 1], top, None, ALU.mult).then_inc(s_sm, 1)
                dve.wait_ge(s_sm, 3 * count)

            def set_scale(u):
                scale_of(u, W_TOP, u + 2)
                V.tensor_scalar(inv[:, u:u + 1], mx[:, u:u + 1], mx[:, U:U + 1],
                                LN_BOUND / (W_TOP * H_TOP), ALU.mult, ALU.mult).then_inc(s_wsc, 1)

            def lo_unit(u):
                dve.wait_ge(s_whi, u + 1)
                if u >= UO:
                    wait_lo(dve, UG + 1)
                V.scalar_tensor_tensor(unit(w_lo, u), stage[u % 4], sw[:, u:u + 1], unit(w_hi, u),
                                       ALU.mult, ALU.subtract).then_inc(s_wlo, 1)

            def norm_stats(j, src, st, mv, s_bn, s_ag):
                after(dve, s_ag, j)
                for g in range(2):
                    last = V.bn_stats(st[:, 6 * g:6 * g + 6], src[:, g * HALF:(g + 1) * HALF])
                last.then_inc(s_bn, 1)
                dve.wait_ge(s_cv, 8)
                dve.wait_ge(s_bn, j + 1)
                V.bn_aggr(mv, st).then_inc(s_ag, 1)

            def recurrence_terms(n, done, dst, first):
                for g in range(2):
                    dve.wait_ge(done, 3 * n + g + 2)
                    V.tensor_tensor(dst[:, g * HALF:(g + 1) * HALF].rearrange("p (c n) -> p c n", n=P),
                                    ps_t[g][:, :].rearrange("p (c n) -> p c n", n=P),
                                    per_chunk(eu, 4 * g, 4 * g + 4, P), ALU.mult).then_inc(first, 1)

            def scan(n, scanned, carry, saved):
                V.tensor_tensor_scan(seg[:, :], decay[:, :], seg[:, :], 0.0, ALU.mult, ALU.add).then_inc(scanned, 1)
                dve.wait_ge(scanned, n + 1)
                V.tensor_copy(carry[:, :], seg_rows[:, :, TT]).then_inc(saved, 1)
                if isinstance(n, int) and n == 0:
                    V.tensor_copy(seg_rows[:, :, 0], seg_rows[:, :, 1]).then_inc(s_y0, 1)
                    dve.wait_ge(s_y0, 1 if carry is carry_b else 2)

            def add_state(dst, done):
                V.tensor_tensor(tok(dst), tok(dst), seg4(0, TT), ALU.add).then_inc(done, 1)

            def step(i, slot, main, nxt, nxt2, prev):
                n, p = i + 1, i - 1
                o_h = by_head(o_sb, DV)
                if prev:
                    dve.wait_ge(s_o, 4 * (p + 1))
                    after(dve, s_oc, p)
                    V.tensor_reduce(osum, o_h, AX_X, ALU.add).then_inc(s_os, 1)
                    dve.wait_ge(s_os, p + 1)
                    V.tensor_scalar(osum, osum, 1.0 / DV, None, ALU.mult).then_inc(s_os2, 1)
                    dve.wait_ge(s_os2, p + 1)
                    V.tensor_tensor(o_h, o_h, per_head(osum, 0, H, DV), ALU.subtract).then_inc(s_oc, 1)
                if nxt:
                    denominator_scan(n)
                if prev:
                    dve.wait_ge(s_sq, p + 1)
                    V.tensor_reduce(ossq, by_head(squares, DV), AX_X, ALU.add).then_inc(s_ss, 1)
                if nxt:
                    denominator_add(n)
                if prev:
                    gate_scale(p)
                if main:
                    dve.wait_ge(s_q, i + 1)
                    after(dve, s_op, 4 * i)
                    after(dve, s_o, 4 * i)
                    rotate(dve, V, i, 0, q_sb, rot_q, s_r1q, s_rq)
                if nxt:
                    numerator(n)
                if prev:
                    dve.wait_ge(s_f, p + 1)
                    dve.wait_ge(s_og, p + 1)
                    V.tensor_tensor(o_h, o_h, per_head(fac, 0, H, DV), ALU.mult).then_inc(s_gt, 1)
                if nxt:
                    recurrence_output(n, 0)
                if prev:
                    for g in range(2):
                        dve.wait_ge(s_gthi, 2 * p + g + 1)
                        part = slice(g * HALF, (g + 1) * HALF)
                        V.tensor_tensor(gt_lo[:, part], ps_t[g][:, :], gt_hi[:, part], ALU.subtract)\
                         .then_inc(s_gtlo, 1)
                if nxt:
                    recurrence_output(n, 1)
                if main:
                    for g in range(2):
                        dve.wait_ge(s_vr, 2 * i + g + 1)
                        V.tensor_reduce(delta[:, g * 8:(g + 1) * 8], by_head(tmp[:, g * HALF:(g + 1) * HALF], DV),
                                        AX_X, ALU.add).then_inc(s_dl, 1)
                    dve.wait_ge(s_dl, 2 * (i + 1))
                    after(dve, s_sv, i)
                    V.tensor_scalar(sgn, delta, 0.0, 2.0, ALU.is_ge, ALU.mult).then_inc(s_ob, 1)
                    dve.wait_ge(s_ob, 5 * i + 1)
                    V.tensor_scalar(sgn, sgn, -1.0, None, ALU.add).then_inc(s_sgn, 1)
                if nxt:
                    residual(n, (slot + 1) % 3)
                if prev:
                    dve.wait_ge(s_us, p + 1)
                    final(p, 0, (slot + 2) % 3)
                if main:
                    dve.wait_ge(s_cump, i + 1)
                    after(dve, s_cf, i)
                    V.tensor_tensor(ctmp, ps_s[0][:, 0:H], sgn, ALU.mult).then_inc(s_cum, 1)
                    dve.wait_ge(s_cum, i + 1)
                    V.tensor_scalar(ctmp, ctmp, cnt_c[:, :], None, ALU.add).then_inc(s_pr, 1)
                    dve.wait_ge(s_pr, 3 * i + 1)
                    V.reciprocal(ctmp, ctmp).then_inc(s_pr, 1)
                    dve.wait_ge(s_th, 2 * (i + 1))
                    V.tensor_scalar(pr, pr, 0.5 * DK ** -0.5, 0.5 * DK ** -0.5, ALU.mult, ALU.add).then_inc(s_pr, 1)
                    dve.wait_ge(s_pr, 3 * (i + 1))
                    V.tensor_tensor(coef, pr, ctmp, ALU.mult).then_inc(s_cf, 1)
                if prev:
                    final(p, 1, (slot + 2) % 3)
                if main:
                    q_block(i, 0)
                    q_block(i, 1)
                if nxt:
                    conv_products(n, 0)
                if main:
                    mask(i, 0)
                    q_block(i, 2)
                if nxt:
                    conv_products(n, 1)
                if main:
                    mask(i, 1)
                    q_block(i, 3)
                if nxt:
                    conv_sum(n)
                if main:
                    head_out(i, 0)
                    mask(i, 2)
                    head_out(i, 1)
                    mask(i, 3)
                if nxt2:
                    first_norm(i + 2, (slot + 2) % 3)
                if nxt:
                    h_low(n)
                if main:
                    head_out(i, 2)
                    head_out(i, 3)

            def final(p, g, slot):
                part = slice(g * HALF, (g + 1) * HALF)
                dve.wait_ge(s_up, 2 * p + g + 1)
                V.scalar_tensor_tensor(x_ring[:, slot, part], ps_g[g][:, :], usc[:, g:g + 1], x_ring[:, slot, part],
                                       ALU.mult, ALU.add).then_inc(s_fin, 1)

            def denominator_scan(n):
                after(dve, s_hlo, 2 * n)
                recurrence_terms(n, s_sega, fa, s_fda)
                scan(n, s_sca, carry_b, s_sva)

            def denominator_add(n):
                dve.wait_ge(s_fda, 2 * n + 2)
                add_state(fa, s_den)

            def numerator(n):
                after(dve, s_yp, 2 * n)
                recurrence_terms(n, s_segb, fb, s_fdb)
                scan(n, s_scb, carry_a, s_svb)
                dve.wait_ge(s_fdb, 2 * n + 2)
                add_state(fb, s_num)

            def recurrence_output(n, g):
                part = slice(g * HALF, (g + 1) * HALF)
                dve.wait_ge(s_den, n + 1)
                V.reciprocal(fa[:, part], fa[:, part]).then_inc(s_rec, 1)
                dve.wait_ge(s_num, n + 1)
                dve.wait_ge(s_rec, 2 * n + g + 1)
                V.tensor_tensor(fb[:, part], fb[:, part], fa[:, part], ALU.mult).then_inc(s_y, 1)

            def residual(n, slot):
                xs = x_ring[:, slot, :]
                for g in range(2):
                    dve.wait_ge(s_yp, 2 * n + g + 1)
                    part = slice(g * HALF, (g + 1) * HALF)
                    V.scalar_tensor_tensor(xs[:, part], ps_t[g][:, :], tg[:, 0:1], xs[:, part],
                                           ALU.mult, ALU.add).then_inc(s_x2, 1)
                dve.wait_ge(s_x2, 2 * (n + 1))
                norm_stats(n, xs, st2, mv2, s_bn2, s_ag2)

            def conv_sum(n):
                dve.wait_ge(s_z, 2 * (n + 1))
                dve.wait_ge(s_z2, 2 * (n + 1))
                V.tensor_tensor(tok(fa[:, :])[:, :, :, 1:NB], tok(fa[:, :])[:, :, :, 1:NB],
                                tok(seg[:, 0:C])[:, :, :, 0:NB - 1], ALU.add).then_inc(s_pre, 1)

            def h_low(n):
                for g in range(2):
                    dve.wait_ge(s_hhi, 2 * n + g + 1)
                    part = slice(g * HALF, (g + 1) * HALF)
                    V.scalar_tensor_tensor(h_lo[:, part], fa[:, part], sw[:, U:U + 1], h_hi[:, part],
                                           ALU.mult, ALU.subtract).then_inc(s_hlo, 1)

            def conv_products(n, g):
                dve.wait_ge(s_y, 2 * n + 2)
                dve.wait_ge(s_xnp, 2 * n + g + 1)
                V.tensor_tensor(fa[:, g * HALF:(g + 1) * HALF].rearrange("p (c n) -> p c n", n=P),
                                ps_t[g][:, :].rearrange("p (c n) -> p c n", n=P),
                                per_chunk(cw1, 4 * g, 4 * g + 4, P), ALU.mult).then_inc(s_z, 1)
                V.tensor_tensor(seg[:, g * HALF:(g + 1) * HALF].rearrange("p (c n) -> p c n", n=P),
                                ps_t[g][:, :].rearrange("p (c n) -> p c n", n=P),
                                per_chunk(cw0, 4 * g, 4 * g + 4, P), ALU.mult).then_inc(s_z2, 1)

            def mask(i, g):
                dve.wait_ge(s_sp, 4 * i + g + 1)
                after(dve, s_op, 4 * i + g - 1)
                if g < 2:
                    dve.wait_ge(s_ktp, i + 1)
                V.tensor_tensor(probs[g % 2].rearrange("p (h l) -> p h l", h=HG),
                                ps_s[g % 2][:, :].rearrange("p (h l) -> p h l", h=HG),
                                causal_m[:, :].rearrange("p (o l) -> p o l", o=1)
                                .to_broadcast([P, HG, P]), ALU.mult).then_inc(s_p, 1)

            def gate_scale(i):
                dve.wait_ge(s_sg, 2 * (i + 1))
                after(dve, s_us, i)
                V.tensor_reduce(gmx, sg, AX_X, ALU.max, apply_absolute_value=True).then_inc(s_gm, 1)
                dve.wait_ge(s_gm, i + 1)
                V.tensor_scalar(gmx, gmx, TINY, None, ALU.max).then_inc(s_gm2, 1)
                dve.wait_ge(s_gm2, i + 1)
                after(dve, s_gs, i)
                V.reciprocal(grc, gmx).then_inc(s_rg, 1)
                after(dve, s_fin, 2 * i)
                V.tensor_scalar(usc, base, gmx, HEAD_BOUND / G_TOP, ALU.mult, ALU.mult).then_inc(s_us, 1)
                dve.wait_ge(s_rg, i + 1)
                V.tensor_scalar(gsc, grc, G_TOP / HEAD_BOUND, None, ALU.mult).then_inc(s_gs, 1)

            def first_norm(j, slot):
                dve.wait_ge(s_x, 16 * (j + 1))
                norm_stats(j, x_ring[:, slot, :], st1, mv1, s_bn1, s_ag1)

            def q_block(i, g):
                dve.wait_ge(s_qt, i + 1)
                after(dve, s_sp, 4 * i + g - 1)
                if g < 2:
                    after(dve, s_up, 2 * i)
                V.tensor_tensor(q_blk[g % 2].rearrange("p (h l) -> p h l", h=HG),
                                q_sb[:, g * P:(g + 1) * P].rearrange("p (o l) -> p o l", o=1)
                                .to_broadcast([P, HG, P]),
                                head_m[:, :].rearrange("p (h o) -> p h o", o=1).to_broadcast([P, HG, P]),
                                ALU.mult).then_inc(s_qb, 1)

            def head_out(i, g):
                dve.wait_ge(s_op, 4 * i + g + 1)
                after(dve, s_gtp, 2 * i)
                both = ps_o[g % 2][:, :].rearrange("p (h s d) -> p h s d", h=HG, s=2)
                part = by_head(tmp[:, g * HG * DV:(g + 1) * HG * DV], DV)
                V.tensor_tensor(part, both[:, :, 1, :], per_head(sgn, g * HG, (g + 1) * HG, DV), ALU.mult)\
                 .then_inc(s_ob, 1)
                dve.wait_ge(s_ob, 5 * i + g + 2)
                V.tensor_tensor(by_head(o_sb[:, g * HG * DV:(g + 1) * HG * DV], DV), both[:, :, 0, :], part,
                                ALU.add).then_inc(s_o, 1)

            for cols, value in ((nhalf, -0.5), (eps_c, EPS), (dv_c, 1.0 / DV), (shift1, -SHIFT), (shift2, 0.0)):
                V.memset(cols, value).then_inc(s_cv, 1)
            V.memset(carry_a[:, :], 0.0).then_inc(s_cv, 1)
            V.memset(carry_b[:, :], 0.0).then_inc(s_cv, 1)
            V.memset(decay[:, :], 0.0).then_inc(s_cv, 1)
            dve.wait_ge(s_const, 16 * 7)
            V.tensor_scalar(eu, eu, U_MAX, None, ALU.min).then_inc(s_cv, 1)
            first_norm(0, 0)
            dve.wait_ge(s_cv, 9)
            dve.wait_ge(s_ca, 6)
            V.tensor_copy(decay[:, :].rearrange("p (c b t) -> p c b t", c=KC, b=NB)[:, :, :, 1:SEG],
                          dk.rearrange("p (c o q) -> p c o q", o=1, q=1).to_broadcast([P, KC, NB, TT]))\
             .then_inc(s_cv, 1)
            V.tensor_tensor(delta[:, 0:KC], delta[:, 0:KC], sgn[:, 0:KC], ALU.add).then_inc(s_cv, 1)
            dve.wait_ge(s_cv, 11)
            V.tensor_reduce(mx[:, U:U + 1], delta[:, 0:KC], AX_X, ALU.max).then_inc(s_cwmax, 1)
            scale_of(U, H_TOP / LN_BOUND, 1)
            denominator_scan(0)
            denominator_add(0)
            numerator(0)
            set_scale(0)
            recurrence_output(0, 0)
            recurrence_output(0, 1)
            set_scale(1)
            lo_unit(0)
            residual(0, 0)
            set_scale(2)
            lo_unit(1)
            set_scale(3)
            conv_products(0, 0)
            conv_products(0, 1)
            conv_sum(0)
            first_norm(1, 1)
            set_scale(4)
            lo_unit(2)
            h_low(0)
            lo_unit(3)
            set_scale(5)
            lo_unit(4)
            dve.wait_ge(s_router, 16 * 7)
            V.tensor_tensor(router_d[:, :], router_d[:, :], x_ring[:, 2, :], ALU.subtract).then_inc(s_base, 1)
            lo_unit(5)
            set_scale(6)
            lo_unit(6)
            set_scale(7)
            for g in range(2):
                V.tensor_scalar(base[:, g:g + 1], mx[:, UO + g:UO + g + 1], tg[:, 1:2], 1.0 / W_TOP,
                                ALU.mult, ALU.mult).then_inc(s_base, 1)
            lo_unit(7)
            dve.wait_ge(s_base, 3)
            pipeline(dve, step)

        @block.gpsimd
        def _(pool):
            G = nc.gpsimd
            U = len(UNITS)

            def bound_all(u, s, count):
                pool.wait_ge(s, count)
                G.partition_all_reduce(mx[:, u:u + 1], mx[:, u:u + 1], P, AMAX).then_inc(s_wall, 1)

            def norm_scale(j, mv, ve, rs, nm, nb, shift, s_ag, s_rs, s_nb):
                pool.wait_ge(s_ag, j + 1)
                G.tensor_tensor(ve, mv[:, 1:2], eps_c[:, 0:1], ALU.add).then_inc(s_rs, 1)
                pool.wait_ge(s_rs, 3 * j + 1)
                G.tensor_tensor(rs, ve, nhalf[:, 0:1], ALU.pow).then_inc(s_rs, 1)
                pool.wait_ge(s_rs, 3 * j + 2)
                after(pool, s_nb, j)
                G.tensor_tensor(nm, mv[:, 0:1], rs, ALU.mult).then_inc(s_rs, 1)
                pool.wait_ge(s_rs, 3 * j + 3)
                G.tensor_tensor(nb, shift, nm, ALU.subtract).then_inc(s_nb, 1)

            def first_scale(j):
                norm_scale(j, mv1, ve1, rs1, nm1, nb1, shift1, s_ag1, s_rs1, s_nb1)

            def second_scale(j):
                norm_scale(j, mv2, ve2, rs2, nm2, nb2, shift2, s_ag2, s_rs2, s_nb2)

            def exp_kv(j):
                pool.wait_ge(s_e, j + 1)
                pool.wait_ge(s_vl, 16 * (j + 1))
                G.tensor_tensor(vx[:, :], vx[:, :], ek[:, :], ALU.mult).then_inc(s_ev, 1)

            def head_factors(p):
                pool.wait_ge(s_ss, p + 1)
                pool.wait_ge(s_cf, p + 1)
                G.tensor_tensor(ftmp, coef, coef, ALU.mult).then_inc(s_fp, 1)
                pool.wait_ge(s_fp, 6 * p + 1)
                G.tensor_tensor(ftmp, ftmp, ossq, ALU.mult).then_inc(s_fp, 1)
                pool.wait_ge(s_fp, 6 * p + 2)
                G.tensor_tensor(ftmp, ftmp, dv_c, ALU.mult).then_inc(s_fp, 1)
                pool.wait_ge(s_fp, 6 * p + 3)
                G.tensor_tensor(ftmp, ftmp, eps_c, ALU.add).then_inc(s_fp, 1)
                pool.wait_ge(s_fp, 6 * p + 4)
                G.tensor_tensor(fac, ftmp, nhalf, ALU.pow).then_inc(s_fp, 1)
                pool.wait_ge(s_fp, 6 * p + 5)
                G.tensor_tensor(fac, fac, coef, ALU.mult).then_inc(s_fp, 1)
                pool.wait_ge(s_fp, 6 * p + 6)
                pool.wait_ge(s_gs, p + 1)
                G.tensor_tensor(fac, fac, gsc.to_broadcast([P, H]), ALU.mult).then_inc(s_f, 1)

            def step(i, slot, main, nxt, nxt2, prev):
                n, p = i + 1, i - 1
                if prev:
                    pool.wait_ge(s_sq, p + 1)
                    pool.wait_ge(s_sg, 2 * (p + 1))
                    G.tensor_tensor(o_sb, o_sb, sg, ALU.mult).then_inc(s_og, 1)
                if prev:
                    head_factors(p)
                if main:
                    pool.wait_ge(s_k, i + 1)
                    after(pool, s_op, 4 * i)
                    after(pool, s_o, 4 * i)
                    rotate(pool, G, i, 1, k_sb, rot_k, s_r1k, s_rk)
                    pool.wait_ge(s_rk, i + 1)
                    pool.wait_ge(s_rq, i + 1)
                    for g in range(2):
                        pool.wait_ge(s_vc, 2 * i + g + 1)
                        G.tensor_tensor(by_head(tmp[:, g * HALF:(g + 1) * HALF], DV), v2[:, g * 8:(g + 1) * 8, 0, :],
                                        by_head(router_d[:, g * HALF:(g + 1) * HALF], DV), ALU.mult)\
                         .then_inc(s_vr, 1)
                if nxt:
                    second_scale(n)
                if main:
                    pool.wait_ge(s_sgn, i + 1)
                    G.tensor_tensor(v2[:, :, 1, :], v2[:, :, 0, :], per_head(sgn, 0, H, DV), ALU.mult)\
                     .then_inc(s_sv, 1)
                if nxt2:
                    first_scale(i + 2)
                if nxt2:
                    exp_kv(i + 2)

            pool.wait_ge(s_cv, 8)
            first_scale(0)
            bound_all(U, s_cwmax, 1)
            exp_kv(0)
            for u in range(4):
                bound_all(u, s_wsum, u + 1)
            second_scale(0)
            bound_all(4, s_wsum, 5)
            first_scale(1)
            bound_all(5, s_wsum, 6)
            exp_kv(1)
            bound_all(6, s_wsum, 7)
            bound_all(7, s_wsum, 8)
            pool.wait_ge(s_router, 16 * 7)
            pool.wait_ge(s_base, 1)
            pipeline(pool, step)


_INPUTS = ("x", "ctx_2048", "g_xattn", "g_ffn", "decay", "first", "conv", "wq", "wk", "wv", "wg", "router", "wout",
           "identity", "causal", "cos", "sin", "count", "heads")


def _shape_constants():
    import numpy as np

    f = np.float32
    t, b = np.arange(P) // NB, np.arange(P) % NB
    inv_freq = (f(1.0) / f(10000.0) ** (np.arange(0, DK, 2, dtype=f) / f(DK))).astype(f)
    angle = b.astype(f)[:, None] * inv_freq[None, :]
    cos, sin = np.cos(angle).astype(f), np.sin(angle).astype(f)
    return {
        "identity": np.eye(P, dtype=f),
        "causal": ((t[:, None] == t[None, :]) & (b[:, None] <= b[None, :])).astype(f),
        "cos": np.concatenate([cos, cos], axis=1),
        "sin": np.concatenate([-sin, sin], axis=1),
        "count": (b + 1).astype(f)[:, None],
        "heads": (np.arange(P)[:, None] // DK == np.arange(HG)[None, :]).astype(f),
    }


def kernel(**inputs):
    import numpy as np
    import concourse.bacc as bacc
    from concourse.bass_utils import run_bass_kernel_spmd

    a = {n: np.asarray(v) for n, v in inputs.items()}
    layout = {
        "x": a["x"], "ctx_2048": a["ctx_2048"],
        "g_xattn": a["g_xattn"].reshape(1, 1), "g_ffn": a["g_ffn"].reshape(1, 1),
        "decay": a["L0_xattn_time_decay"].reshape(KC, P).T, "first": a["L0_xattn_time_first"].reshape(KC, P).T,
        "conv": a["L0_ffn_conv_w"].reshape(KC, P, 2).transpose(2, 1, 0),
        "wq": a["L0_ffn_Wq"], "wk": a["L0_ffn_Wk"], "wv": a["L0_ffn_Wv"], "wg": a["L0_ffn_Wg"],
        "router": a["L0_ffn_router_w"].reshape(C, 2).T, "wout": a["L0_ffn_Wout"],
        **_shape_constants(),
    }
    nc = bacc.Bacc("TRN2", target_bir_lowering=False, num_devices=1)
    arrays, args = {}, []
    for name in _INPUTS:
        arr = np.ascontiguousarray(layout[name])
        arrays[f"in_{name}"] = arr
        args.append(nc.dram_tensor(f"in_{name}", arr.shape, mybir.dt.from_np(arr.dtype), kind="ExternalInput").ap())
    out = nc.dram_tensor("out", a["x"].shape, F32, kind="ExternalOutput").ap()
    flamingo_layer(nc, *args, out)
    r = run_bass_kernel_spmd(nc, [arrays], core_ids=[0])
    return r.results[0]["out"]
```

```python
from contextlib import ExitStack

import concourse.bass as bass
from concourse import mybir

F32 = mybir.dt.float32
F16 = mybir.dt.float16
BF16 = mybir.dt.bfloat16
ALU = mybir.AluOpType
ACT = mybir.ActivationFunctionType
AX_X = mybir.AxisListType.X
AMAX = bass.bass_isa.ReduceOp.max

P = 128
NB = 8
TT = P // NB
SEG = TT + 1
C = 1024
KC = C // P
SQ = 32
CB = C // SQ
BB = SQ // TT
HALF = C // 2
H = 16
DK = 32
DV = 64
HG = 4
NG = H // HG
EPS = 1e-5
SHIFT = 40.0
U_MAX = 87.0
TINY = 1e-30
LN_BOUND = float(C) ** 0.5
HEAD_BOUND = float(DV) ** 0.5
W_TOP = 2.0 ** 14
H_TOP = 2.0 ** 15
G_TOP = 2.0 ** 14
UNITS = ("q", "k", "v0", "v1", "g0", "g1", "o0", "o1")
UQ, UK, UV, UG, UO = 0, 1, 2, 4, 6


def flamingo_layer(nc, x, ctxt, g_xattn, g_ffn, decay_cols, first_cols, conv_cols, w_q, w_k, w_v, w_g,
                   router, w_out, identity, causal, cos_rows, sin_rows, count_rows, head_rows, out):
    T = x.shape[1]
    N = T // TT
    LOOPED = (N - 3) // 3 * 3
    w_src = [w_q, w_k, w_v[:, 0:HALF], w_v[:, HALF:C], w_g[:, 0:HALF], w_g[:, HALF:C],
             w_out[:, 0:HALF], w_out[:, HALF:C]]

    with ExitStack() as ctx:
        def sb(name, shape, dt=F32):
            return ctx.enter_context(nc.sbuf_tensor(name, shape, dt))

        def bank(name):
            return ctx.enter_context(nc.psum_tensor(name, [P, HALF], F32))

        def sem(name):
            return ctx.enter_context(nc.semaphore(name))

        w_hi = sb("w_hi", [P, len(UNITS), KC, HALF], F16)
        w_lo = sb("w_lo", [P, len(UNITS), KC, HALF], F16)
        x_ring = sb("x_ring", [P, 3, C])
        vx = sb("vx", [P, C])
        ek = sb("ek", [P, C])
        decay = sb("decay", [P, CB * BB * SEG])
        seg = sb("seg", [P, CB * BB * SEG])
        fa = sb("fa", [P, C])
        fb = sb("fb", [P, C])
        h_hi = sb("h_hi", [P, C], F16)
        h_lo = sb("h_lo", [P, C], F16)
        work = sb("work", [P, 2, KC * HALF])
        v2 = work[:, 0, 0:2 * C].rearrange("p (h s d) -> p h s d", h=H, s=2)
        sg = work[:, 0, 2 * C:3 * C]
        o_sb = work[:, 0, 3 * C:4 * C]
        q_sb = work[:, 1, 0:HALF]
        k_sb = work[:, 1, HALF:C]
        rot_q = work[:, 1, C:C + HALF]
        rot_k = work[:, 1, C + HALF:2 * C]
        probs = (rot_q, rot_k)
        g_split = work[:, 1, 2 * C:3 * C].bitcast(F16)
        gt_hi, gt_lo = g_split[:, 0:C], g_split[:, C:2 * C]
        q_blk = (work[:, 1, 2 * C:2 * C + HALF], work[:, 1, 2 * C + HALF:3 * C])
        squares = work[:, 1, 2 * C:3 * C]
        tmp = work[:, 1, 3 * C:4 * C]
        router_d = sb("router_d", [P, C])
        ident = sb("ident", [P, P])
        causal_m = sb("causal_m", [P, P])
        cos2 = sb("cos2", [P, DK])
        sin2 = sb("sin2", [P, DK])
        cnt_c = sb("cnt_c", [P, 1])
        head_m = sb("head_m", [P, HG])
        small = sb("small", [P, 370])
        at = [0]

        def col(n):
            at[0] += n
            return small[:, at[0] - n:at[0]]

        dk = col(CB)
        eu = col(CB)
        cw0, cw1 = col(KC), col(KC)
        mx = col(len(UNITS) + 1)
        sw = col(len(UNITS) + 1)
        inv = col(len(UNITS))
        tg = col(2)
        base = col(2)
        nhalf = col(H)
        eps_c, dv_c = col(H), col(H)
        shift1, shift2 = col(1), col(1)
        st1, st2 = col(12), col(12)
        mv1, mv2 = col(2), col(2)
        ve1, ve2 = col(1), col(1)
        rs1, rs2 = col(1), col(1)
        nm1, nm2 = col(1), col(1)
        nb1, nb2 = col(1), col(1)
        delta = col(H)
        sgn = col(H)
        pr = col(H)
        coef = col(H)
        ctmp = col(H)
        osum = col(H)
        ossq = col(H)
        ftmp = col(H)
        fac = col(H)
        gmx = col(1)
        grc = col(1)
        gsc = col(1)
        usc = col(2)
        carry_b = sb("carry_b", [P, CB * BB])
        carry_a = sb("carry_a", [P, CB * BB])

        ps_t = (bank("ps_t0"), bank("ps_t1"))
        ps_g = (bank("ps_g0"), bank("ps_g1"))
        ps_s = (bank("ps_s0"), bank("ps_s1"))
        ps_o = (bank("ps_o0"), bank("ps_o1"))

        s_const, s_w = sem("const_loaded"), [sem(f"weight_loaded{n}") for n in range(4)]
        s_x, s_vl, s_store = sem("x_loaded"), sem("v_loaded"), sem("out_stored")
        s_max, s_wsum, s_wall, s_wsc, s_whi, s_wlo = (sem(n) for n in
            ("max_done", "wsum_done", "wbound_all", "wscale_done", "whi_done", "wlo_done"))
        s_router, s_base, s_wpart = sem("router_loaded"), sem("base_done"), sem("wsum_part")
        s_ca, s_cv = sem("const_act"), sem("const_dve")
        s_xnp = sem("xn_transposed")
        s_ekt, s_evt, s_yt = sem("ek_transposed"), sem("ev_transposed"), sem("y_transposed")
        s_qp, s_kp, s_vp, s_gp, s_up = sem("q_proj"), sem("k_proj"), sem("v_proj"), sem("g_proj"), sem("out_proj")
        s_qtp, s_ktp, s_gtp = sem("q_transposed"), sem("k_transposed"), sem("gated_transposed")
        s_cump, s_sp, s_op = sem("cum_matmul"), sem("scores_matmul"), sem("o_matmul")
        s_bn1, s_ag1, s_rs1, s_nb1, s_e, s_ev = (sem(n) for n in
            ("bn1", "aggr1", "rstd1", "nbias1", "ek_done", "ev_done"))
        s_fda, s_fdb = sem("first_den"), sem("first_num")
        s_sca, s_scb, s_sva, s_svb = sem("scan_den"), sem("scan_num"), sem("save_den"), sem("save_num")
        s_den, s_num, s_rec, s_y, s_x2 = (sem(n) for n in
            ("den_done", "num_done", "recip_done", "y_done", "x2_done"))
        s_bn2, s_ag2, s_rs2, s_nb2, s_xn = (sem(n) for n in
            ("bn2", "aggr2", "rstd2", "nbias2", "xn_done"))
        s_z, s_z2, s_pre, s_h, s_hhi, s_hlo = (sem(n) for n in
            ("conv_now", "conv_past", "conv_done", "h_done", "h_hi_done", "h_lo_done"))
        s_q, s_k, s_vc = sem("q_copied"), sem("k_copied"), sem("v_copied")
        s_r1q, s_r1k, s_rq, s_rk = sem("rot_q_part"), sem("rot_k_part"), sem("rot_q"), sem("rot_k")
        s_qt, s_kt = sem("qt_copied"), sem("kt_copied")
        s_vr, s_dl = sem("v_router"), sem("delta_done")
        s_sgn, s_sv, s_th, s_pr, s_cum, s_cf = (sem(n) for n in
            ("sign_done", "signed_v", "tanh_done", "prob_done", "cum_done", "coef_done"))
        s_sm = sem("dve_small")
        s_qb, s_p, s_ob, s_o = sem("q_block"), sem("probs_done"), sem("o_part"), sem("o_done")
        s_os, s_oc, s_sq, s_ss = sem("o_sum"), sem("o_centred"), sem("o_square"), sem("o_var")
        s_os2 = sem("o_mean")
        s_fp, s_f, s_og, s_gt = sem("factor_part"), sem("factor"), sem("o_times_gate"), sem("gated")
        s_gthi, s_gtlo = sem("gt_hi"), sem("gt_lo")
        s_sg, s_gm, s_gm2, s_gs, s_us = (sem(n) for n in
            ("silu_g", "gate_max", "gate_max_guard", "gate_scale", "out_scale"))
        s_fin = sem("final_done")
        s_rg, s_y0 = sem("gate_recip"), sem("first_step_state")

        block = ctx.enter_context(nc.Block())

        flat = "p u k n -> p (u k n)"
        stage = (w_hi[:, UO:UO + 2, :, :].rearrange(flat).bitcast(F32),
                 w_lo[:, UO:UO + 2, :, :].rearrange(flat).bitcast(F32), work[:, 0, :], work[:, 1, :])

        def wait_lo(eng, u):
            eng.wait_ge(s_wlo, u + 1)

        def unit(w, u):
            return w[:, u, :, :].rearrange("p k n -> p (k n)")

        seg_rows = seg[:, :].rearrange("p (s t) -> p s t", t=SEG)

        def cbt(ap):
            return ap.rearrange("p (c b t) -> p c b t", c=CB, b=BB)

        def per_chunk(cols, lo, hi, n):
            return cols[:, lo:hi].rearrange("p (c o) -> p c o", o=1).to_broadcast([P, hi - lo, n])

        def per_head(cols, lo, hi, n):
            return cols[:, lo:hi].rearrange("p (h o) -> p h o", o=1).to_broadcast([P, hi - lo, n])

        def by_head(ap, d):
            return ap.rearrange("p (h d) -> p h d", d=d)

        def after(eng, s, value):
            if not isinstance(value, int) or value > 0:
                eng.wait_ge(s, value)

        def pipeline(eng, step):
            step(0, 0, True, True, True, False)
            with eng.Fori(1, LOOPED + 1, 3) as i:
                for r in range(3):
                    step(i + r, (1 + r) % 3, True, True, True, True)
            for i in range(LOOPED + 1, N - 2):
                step(i, i % 3, True, True, True, True)
            step(N - 2, (N - 2) % 3, True, True, False, True)
            step(N - 1, (N - 1) % 3, True, False, False, True)
            step(N, N % 3, False, False, False, True)

        def rotate(eng, E, i, half_of_tmp, src, dst, parts, done):
            scratch = tmp[:, half_of_tmp * HALF:(half_of_tmp + 1) * HALF]
            s4 = src.rearrange("p (h s d) -> p h s d", h=H, s=2)
            t4 = scratch.rearrange("p (h s d) -> p h s d", h=H, s=2)
            half = DK // 2
            E.tensor_tensor(by_head(dst, DK), by_head(src, DK),
                            cos2[:, :].rearrange("p (o d) -> p o d", o=1).to_broadcast([P, H, DK]), ALU.mult)\
             .then_inc(parts, 1)
            for s in range(2):
                E.tensor_tensor(t4[:, :, s, :], s4[:, :, 1 - s, :],
                                sin2[:, s * half:(s + 1) * half].rearrange("p (o d) -> p o d", o=1)
                                .to_broadcast([P, H, half]), ALU.mult).then_inc(parts, 1)
            eng.wait_ge(parts, 3 * (i + 1))
            E.tensor_tensor(dst, dst, scratch, ALU.add).then_inc(done, 1)

        @block.sync
        def _(sp):
            def load_x(j, slot):
                sp.dma_start(x_ring[:, slot, :], x[:, bass.ds(j * TT, TT), :]).then_inc(s_x, 16)

            def load_v(j):
                sp.dma_start(vx[:, :], ctxt[:, bass.ds(j * TT, TT), :]).then_inc(s_vl, 16)

            def load_unit(u):
                if u >= 4:
                    sp.wait_ge(s_whi, u - 3)
                    wait_lo(sp, u - 4)
                sp.dma_start(stage[u % 4].rearrange("p (k n) -> p k n", k=KC),
                             w_src[u].rearrange("(k p) n -> p k n", p=P)).then_inc(s_w[u % 4], 16)

            load_x(0, 0)
            load_v(0)
            for dst, src in ((dk, decay_cols), (eu, first_cols), (cw0, conv_cols[0]), (cw1, conv_cols[1]),
                             (ident[:, :], identity), (tg[:, 0:1], g_xattn.to_broadcast([P, 1])),
                             (tg[:, 1:2], g_ffn.to_broadcast([P, 1]))):
                sp.dma_start(dst, src).then_inc(s_const, 16)
            load_unit(0)
            load_unit(1)
            load_unit(2)
            load_unit(3)
            load_unit(4)
            sp.wait_ge(s_x, 16)
            load_x(1, 1)
            load_unit(5)
            for dst, src in ((causal_m[:, :], causal), (cos2[:, :], cos_rows), (sin2[:, :], sin_rows),
                             (cnt_c[:, :], count_rows), (head_m[:, :], head_rows),
                             (router_d[:, :], router[0:1, :].to_broadcast([P, C])),
                             (x_ring[:, 2, :], router[1:2, :].to_broadcast([P, C]))):
                sp.dma_start(dst, src).then_inc(s_router, 16)
            sp.wait_ge(s_xnp, 2)
            load_v(1)
            load_unit(6)
            load_unit(7)
            sp.wait_ge(s_wpart, 4)
            sp.wait_ge(s_x, 32)

            def step(i, slot, main, nxt, nxt2, prev):
                if prev:
                    after(sp, s_fin, 2 * i)
                    sp.dma_start(out[:, bass.ds((i - 1) * TT, TT), :], x_ring[:, (slot + 2) % 3, :])\
                      .then_inc(s_store, 16)
                if nxt2:
                    after(sp, s_store, 16 * i)
                    load_x(i + 2, (slot + 2) % 3)
                    after(sp, s_xnp, 2 * (i + 2))
                    load_v(i + 2)

            pipeline(sp, step)
            sp.wait_ge(s_store, 16 * N)

        @block.tensor
        def _(pe):
            def transposes(dst, src, s):
                for n in range(4):
                    last = nc.tensor.transpose(dst[:, n * P:(n + 1) * P], src[:, n * P:(n + 1) * P], ident[:, :])
                last.then_inc(s, 1)

            def project(dst, a_hi, a_lo, u, s, part=None):
                for kc in range(KC) if part is None else range(part * KC // 2, (part + 1) * KC // 2):
                    hi, lo = (a[:, kc * P:(kc + 1) * P] for a in (a_hi, a_lo))
                    nc.tensor.matmul(dst[:, :], hi, w_hi[:, u, kc, :], start=(kc == 0), stop=False)
                    nc.tensor.matmul(dst[:, :], hi, w_lo[:, u, kc, :], start=False, stop=False)
                    last = nc.tensor.matmul(dst[:, :], lo, w_hi[:, u, kc, :], start=False, stop=(kc == KC - 1))
                if part != 0:
                    last.then_inc(s, 1)

            def unit_ready(i, u):
                if isinstance(i, int) and i == 0:
                    pe.wait_ge(s_whi, u + 1)
                    wait_lo(pe, u)

            def step(i, slot, main, nxt, nxt2, prev):
                n, p = i + 1, i - 1
                if main:
                    unit_ready(i, UQ)
                    after(pe, s_hlo, 2 * i + 1)
                    after(pe, s_sg, 2 * i - 1)
                    project(ps_g[0], h_hi, h_lo, UQ, s_qp, 0)
                if main:
                    after(pe, s_hlo, 2 * (i + 1))
                    project(ps_g[0], h_hi, h_lo, UQ, s_qp, 1)
                    unit_ready(i, UK)
                    after(pe, s_sg, 2 * i)
                    project(ps_g[1], h_hi, h_lo, UK, s_kp, 0)
                if main:
                    project(ps_g[1], h_hi, h_lo, UK, s_kp, 1)
                    unit_ready(i, UV)
                    after(pe, s_q, i + 1)
                    project(ps_g[0], h_hi, h_lo, UV, s_vp)
                    after(pe, s_rq, i + 1)
                    after(pe, s_z, 2 * (i + 1))
                    after(pe, s_z2, 2 * (i + 1))
                    transposes(ps_t[0], rot_q, s_qtp)
                    unit_ready(i, UV + 1)
                    after(pe, s_k, i + 1)
                    project(ps_g[1], h_hi, h_lo, UV + 1, s_vp, 0)
                    after(pe, s_rk, i + 1)
                    transposes(ps_t[1], rot_k, s_ktp)
                if prev:
                    for g in range(2):
                        after(pe, s_gt, p + 1)
                        after(pe, s_o, 4 * (p + 1))
                        transposes(ps_o[g], o_sb[:, g * HALF:(g + 1) * HALF], s_gtp)
                if main:
                    project(ps_g[1], h_hi, h_lo, UV + 1, s_vp, 1)
                if prev:
                    for g in range(2):
                        if main:
                            after(pe, s_vc, 2 * i + g + 1)
                        else:
                            after(pe, s_sg, 2 * p + g + 1)
                        for part in range(2):
                            if g == 0:
                                after(pe, s_gtlo, 2 * p + part + 1)
                            project(ps_g[g], gt_hi, gt_lo, UO + g, s_up, part)
                if main and prev:
                    sign_sums(i)
                if nxt and not main:
                    xn_transposes(n, p, main, prev)
                if main:
                    for g in range(2):
                        unit_ready(i, UG + g)
                        if prev:
                            after(pe, s_fin, 2 * p + g + 1)
                        else:
                            after(pe, s_vc, 2 * i + g + 1)
                        for part in range(2):
                            project(ps_g[g], h_hi, h_lo, UG + g, s_gp, part)
                            if (g, part) == (0, 0):
                                if prev:
                                    scores(i, 0)
                                    scores(i, 1)
                                else:
                                    sign_sums(i)
                            elif (g, part) != (1, 1):
                                if (g, part) == (0, 1) and not prev:
                                    scores(i, 0)
                                    scores(i, 1)
                                if (g, part) == (0, 1) and nxt:
                                    xn_transposes(n, p, main, prev)
                                values(i, g)
                                scores(i, g + 2)
                    values(i, 2)
                    values(i, 3)

            def sign_sums(i):
                after(pe, s_sgn, i + 1)
                after(pe, s_p, 4 * i)
                nc.tensor.matmul(ps_s[0][:, 0:H], causal_m[:, :], sgn, start=True, stop=True).then_inc(s_cump, 1)

            def xn_transposes(n, p, main, prev):
                for g in range(2):
                    after(pe, s_xn, 2 * n + g + 1)
                    if main:
                        after(pe, (s_qt, s_kt)[g], n)
                    transposes(ps_t[g], vx[:, g * HALF:(g + 1) * HALF], s_xnp)

            def scores(i, g):
                after(pe, s_qb, 4 * i + g + 1)
                after(pe, s_kt, i + 1)
                after(pe, s_p, 4 * i + g - 1)
                if g == 0:
                    after(pe, s_cum, i + 1)
                nc.tensor.matmul(ps_s[g % 2][:, :], k_sb[:, g * P:(g + 1) * P], q_blk[g % 2],
                                 start=True, stop=True).then_inc(s_sp, 1)

            def values(i, g):
                after(pe, s_p, 4 * i + g + 1)
                after(pe, s_sv, i + 1)
                after(pe, s_o, 4 * i + g - 1)
                if g < 2:
                    after(pe, s_gtlo, 2 * i)
                for h in range(HG):
                    last = nc.tensor.matmul(ps_o[g % 2][:, h * P:(h + 1) * P], probs[g % 2][:, h * P:(h + 1) * P],
                                            v2[:, g * HG + h, :, :].rearrange("p s d -> p (s d)"),
                                            start=True, stop=True)
                last.then_inc(s_op, 1)

            pe.wait_ge(s_const, 16 * 7)
            step(-1, 2, False, True, True, False)
            pipeline(pe, step)

        @block.scalar
        def _(act):
            A = nc.scalar.activation
            act.wait_ge(s_const, 16 * 7)
            A(dk, dk, ACT.Exp).then_inc(s_ca, 1)
            act.wait_ge(s_ca, 1)
            A(dk, dk, ACT.Exp, scale=-1.0).then_inc(s_ca, 1)
            act.wait_ge(s_cv, 9)
            A(eu, eu, ACT.Exp).then_inc(s_ca, 1)
            A(tg, tg, ACT.Tanh).then_inc(s_ca, 1)
            A(delta[:, 0:KC], cw0, ACT.Abs).then_inc(s_ca, 1)
            A(sgn[:, 0:KC], cw1, ACT.Abs).then_inc(s_ca, 1)

            def bound_unit(u):
                act.wait_ge(s_w[u % 4], 16 * (u // 4 + 1))
                if u < UO:
                    A(unit(w_hi, u).bitcast(BF16), stage[u % 4], ACT.Abs, accum_out=mx[:, u:u + 1])\
                     .then_inc(s_wsum, 1)
                    return
                act.wait_ge(s_base, 1)
                free = x_ring[:, 2, :].bitcast(BF16)
                for g in range(2):
                    after(act, s_wpart, 2 * (u - UO) + g)
                    A(free, stage[u % 4][:, g * 2 * C:(g + 1) * 2 * C], ACT.Abs,
                      accum_out=osum[:, 2 * (u - UO) + g:2 * (u - UO) + g + 1]).then_inc(s_wpart, 1)

            def split_unit(u):
                act.wait_ge(s_wsc, u + 1)
                if u >= UO:
                    wait_lo(act, UG)
                A(unit(w_hi, u), stage[u % 4], ACT.Copy, scale=sw[:, u:u + 1]).then_inc(s_whi, 1)

            def exp_k(j, slot):
                act.wait_ge(s_nb1, j + 1)
                after(act, s_ekt, 2 * j)
                after(act, s_ev, j)
                for g in range(2):
                    part = slice(g * HALF, (g + 1) * HALF)
                    A(ek[:, part], x_ring[:, slot, part], ACT.Exp, scale=rs1, bias=nb1).then_inc(s_e, 1)

            def step(i, slot, main, nxt, nxt2, prev):
                n, p = i + 1, i - 1
                if prev:
                    after(act, s_oc, p + 1)
                    after(act, s_sp, 4 * (p + 1))
                    A(squares, o_sb, ACT.Square).then_inc(s_sq, 1)
                if main:
                    if isinstance(i, int) and i == 0:
                        wait_lo(act, UO)
                        wait_lo(act, UO + 1)
                    act.wait_ge(s_qp, i + 1)
                    after(act, s_qb, 4 * i)
                    A(q_sb, ps_g[0][:, :], ACT.Silu, scale=inv[:, UQ:UQ + 1]).then_inc(s_q, 1)
                    act.wait_ge(s_kp, i + 1)
                    after(act, s_sp, 4 * i)
                    A(k_sb, ps_g[1][:, :], ACT.Copy, scale=inv[:, UK:UK + 1]).then_inc(s_k, 1)
                if main:
                    copy_v(i, 0)
                    act.wait_ge(s_qtp, i + 1)
                    A(q_sb, ps_t[0][:, :], ACT.Copy).then_inc(s_qt, 1)
                    act.wait_ge(s_ktp, i + 1)
                    A(k_sb, ps_t[1][:, :], ACT.Copy).then_inc(s_kt, 1)
                if prev:
                    for g in range(2):
                        act.wait_ge(s_gtp, 2 * p + g + 1)
                        act.wait_ge(s_ss, p + 1)
                        A(gt_hi[:, g * HALF:(g + 1) * HALF], ps_o[g][:, :], ACT.Copy).then_inc(s_gthi, 1)
                if main:
                    copy_v(i, 1)
                    act.wait_ge(s_dl, 2 * (i + 1))
                    after(act, s_cf, i)
                    A(pr, delta, ACT.Abs).then_inc(s_th, 1)
                    act.wait_ge(s_th, 2 * i + 1)
                    A(pr, pr, ACT.Tanh, scale=0.5).then_inc(s_th, 1)
                if main:
                    q_block(i, 0)
                    q_block(i, 1)
                if nxt:
                    normed_x(n, (slot + 1) % 3)
                if main:
                    q_block(i, 2)
                    q_block(i, 3)
                    silu_gate(i, 0)
                if nxt:
                    silu_h(n)
                    split_h(n, 0)
                if main:
                    silu_gate(i, 1)
                if nxt:
                    split_h(n, 1)
                if nxt2:
                    exp_k(i + 2, (slot + 2) % 3)

            def normed_x(n, slot):
                act.wait_ge(s_nb2, n + 1)
                act.wait_ge(s_evt, 2 * (n + 1))
                for g in range(2):
                    part = slice(g * HALF, (g + 1) * HALF)
                    A(vx[:, part], x_ring[:, slot, part], ACT.Identity, scale=rs2, bias=nb2).then_inc(s_xn, 1)

            def silu_h(n):
                act.wait_ge(s_pre, n + 1)
                A(fa[:, :], fa[:, :], ACT.Silu).then_inc(s_h, 1)

            def split_h(n, g):
                act.wait_ge(s_h, n + 1)
                after(act, s_gp, 2 * n)
                A(h_hi[:, g * HALF:(g + 1) * HALF], fa[:, g * HALF:(g + 1) * HALF], ACT.Copy,
                  scale=sw[:, len(UNITS):len(UNITS) + 1]).then_inc(s_hhi, 1)

            def q_block(i, g):
                after(act, s_sp, 4 * i + g - 1)
                if g < 2:
                    after(act, s_up, 2 * i)
                act.wait_ge(s_qt, i + 1)
                for h in range(HG):
                    last = A(q_blk[g % 2][:, h * P:(h + 1) * P], q_sb[:, g * P:(g + 1) * P], ACT.Copy,
                             scale=head_m[:, h:h + 1])
                last.then_inc(s_qb, 1)

            def silu_gate(i, g):
                act.wait_ge(s_gp, 2 * i + g + 1)
                after(act, s_og, i)
                after(act, s_gm, i)
                A(sg[:, g * HALF:(g + 1) * HALF], ps_g[g][:, :], ACT.Silu,
                  scale=inv[:, UG + g:UG + g + 1]).then_inc(s_sg, 1)

            def copy_v(i, g):
                act.wait_ge(s_vp, 2 * i + g + 1)
                after(act, s_op, 4 * i)
                A(v2[:, g * 8:(g + 1) * 8, 0, :], by_head(ps_g[g][:, :], DV), ACT.Copy,
                  scale=inv[:, UV + g:UV + g + 1]).then_inc(s_vc, 1)

            exp_k(0, 0)
            bound_unit(0)
            split_unit(0)
            bound_unit(1)
            bound_unit(2)
            split_unit(1)
            bound_unit(3)
            bound_unit(4)
            split_unit(2)
            split_unit(3)
            normed_x(0, 0)
            split_unit(4)
            bound_unit(5)
            split_unit(5)
            silu_h(0)
            split_h(0, 0)
            split_h(0, 1)
            bound_unit(6)
            bound_unit(7)
            split_unit(6)
            split_unit(7)
            exp_k(1, 1)
            pipeline(act, step)

        @block.vector
        def _(dve):
            V = nc.vector
            U = len(UNITS)

            def scale_of(u, top, count):
                dve.wait_ge(s_wall, count)
                V.tensor_scalar(mx[:, u:u + 1], mx[:, u:u + 1], TINY, None, ALU.max).then_inc(s_sm, 1)
                dve.wait_ge(s_sm, 3 * count - 2)
                V.reciprocal(sw[:, u:u + 1], mx[:, u:u + 1]).then_inc(s_sm, 1)
                dve.wait_ge(s_sm, 3 * count - 1)
                V.tensor_scalar(sw[:, u:u + 1], sw[:, u:u + 1], top, None, ALU.mult).then_inc(s_sm, 1)
                dve.wait_ge(s_sm, 3 * count)

            def set_scale(u):
                scale_of(u, W_TOP, u + 2)
                V.tensor_scalar(inv[:, u:u + 1], mx[:, u:u + 1], mx[:, U:U + 1],
                                LN_BOUND / (W_TOP * H_TOP), ALU.mult, ALU.mult).then_inc(s_wsc, 1)

            def lo_unit(u):
                dve.wait_ge(s_whi, u + 1)
                if u >= UO:
                    wait_lo(dve, UG + 1)
                V.scalar_tensor_tensor(unit(w_lo, u), stage[u % 4], sw[:, u:u + 1], unit(w_hi, u),
                                       ALU.mult, ALU.subtract).then_inc(s_wlo, 1)

            def norm_stats(j, src, st, mv, s_bn, s_ag):
                after(dve, s_ag, j)
                for g in range(2):
                    last = V.bn_stats(st[:, 6 * g:6 * g + 6], src[:, g * HALF:(g + 1) * HALF])
                last.then_inc(s_bn, 1)
                dve.wait_ge(s_cv, 8)
                dve.wait_ge(s_bn, j + 1)
                V.bn_aggr(mv, st).then_inc(s_ag, 1)

            def recurrence_terms(n, src, carry, saved, turned, dst, first):
                after(dve, saved, n)
                V.tensor_copy(seg_rows[:, :, 0], carry[:, :]).then_inc(turned, 1)
                V.transpose(seg_rows[:, :, 1:SEG], src).then_inc(turned, 1)
                dve.wait_ge(turned, 2 * (n + 1))
                V.tensor_tensor(cbt(dst), seg_rows[:, :, 1:SEG].rearrange("p (c b) t -> p c b t", b=BB),
                                eu.rearrange("p (c o q) -> p c o q", o=1, q=1).to_broadcast([P, CB, BB, TT]),
                                ALU.mult).then_inc(first, 1)

            def scan(n, first, scanned, carry, saved):
                dve.wait_ge(first, n + 1)
                V.tensor_tensor_scan(seg[:, :], decay[:, :], seg[:, :], 0.0, ALU.mult, ALU.add).then_inc(scanned, 1)
                dve.wait_ge(scanned, n + 1)
                V.tensor_copy(carry[:, :], seg_rows[:, :, TT]).then_inc(saved, 1)
                if isinstance(n, int) and n == 0:
                    V.tensor_copy(seg_rows[:, :, 0], seg_rows[:, :, 1]).then_inc(s_y0, 1)
                    dve.wait_ge(s_y0, 1 if carry is carry_b else 2)

            def add_state(dst, done):
                rows = dst.rearrange("p (s t) -> p s t", t=TT)
                V.tensor_tensor(rows, rows, seg_rows[:, :, 0:TT], ALU.add).then_inc(done, 1)

            def step(i, slot, main, nxt, nxt2, prev):
                n, p = i + 1, i - 1
                o_h = by_head(o_sb, DV)
                if prev:
                    dve.wait_ge(s_o, 4 * (p + 1))
                    after(dve, s_oc, p)
                    V.tensor_reduce(osum, o_h, AX_X, ALU.add).then_inc(s_os, 1)
                    dve.wait_ge(s_os, p + 1)
                    V.tensor_scalar(osum, osum, 1.0 / DV, None, ALU.mult).then_inc(s_os2, 1)
                    dve.wait_ge(s_os2, p + 1)
                    V.tensor_tensor(o_h, o_h, per_head(osum, 0, H, DV), ALU.subtract).then_inc(s_oc, 1)
                if nxt:
                    denominator_terms(n)
                if prev:
                    dve.wait_ge(s_sq, p + 1)
                    V.tensor_reduce(ossq, by_head(squares, DV), AX_X, ALU.add).then_inc(s_ss, 1)
                if nxt:
                    denominator_scan(n)
                if prev:
                    gate_scale(p)
                if main:
                    dve.wait_ge(s_q, i + 1)
                    after(dve, s_op, 4 * i)
                    after(dve, s_o, 4 * i)
                    rotate(dve, V, i, 0, q_sb, rot_q, s_r1q, s_rq)
                if prev:
                    dve.wait_ge(s_f, p + 1)
                    dve.wait_ge(s_og, p + 1)
                    V.tensor_tensor(o_h, o_h, per_head(fac, 0, H, DV), ALU.mult).then_inc(s_gt, 1)
                if nxt:
                    numerator(n)
                if prev:
                    for g in range(2):
                        dve.wait_ge(s_gthi, 2 * p + g + 1)
                        part = slice(g * HALF, (g + 1) * HALF)
                        V.tensor_tensor(gt_lo[:, part], ps_o[g][:, :], gt_hi[:, part], ALU.subtract)\
                         .then_inc(s_gtlo, 1)
                if nxt:
                    recurrence_output(n, 0)
                if nxt:
                    recurrence_output(n, 1)
                if main:
                    for g in range(2):
                        dve.wait_ge(s_vr, 2 * i + g + 1)
                        V.tensor_reduce(delta[:, g * 8:(g + 1) * 8], by_head(tmp[:, g * HALF:(g + 1) * HALF], DV),
                                        AX_X, ALU.add).then_inc(s_dl, 1)
                    dve.wait_ge(s_dl, 2 * (i + 1))
                    after(dve, s_sv, i)
                    V.tensor_scalar(sgn, delta, 0.0, 2.0, ALU.is_ge, ALU.mult).then_inc(s_ob, 1)
                    dve.wait_ge(s_ob, 5 * i + 1)
                    V.tensor_scalar(sgn, sgn, -1.0, None, ALU.add).then_inc(s_sgn, 1)
                if prev:
                    dve.wait_ge(s_us, p + 1)
                    final(p, 0, (slot + 2) % 3)
                if nxt:
                    output_transpose(n)
                if main:
                    dve.wait_ge(s_cump, i + 1)
                    after(dve, s_cf, i)
                    V.tensor_tensor(ctmp, ps_s[0][:, 0:H], sgn, ALU.mult).then_inc(s_cum, 1)
                if nxt:
                    residual(n, (slot + 1) % 3)
                if main:
                    dve.wait_ge(s_cum, i + 1)
                    V.tensor_scalar(ctmp, ctmp, cnt_c[:, :], None, ALU.add).then_inc(s_pr, 1)
                    dve.wait_ge(s_pr, 3 * i + 1)
                    V.reciprocal(ctmp, ctmp).then_inc(s_pr, 1)
                    dve.wait_ge(s_th, 2 * (i + 1))
                    V.tensor_scalar(pr, pr, 0.5 * DK ** -0.5, 0.5 * DK ** -0.5, ALU.mult, ALU.add).then_inc(s_pr, 1)
                    dve.wait_ge(s_pr, 3 * (i + 1))
                    V.tensor_tensor(coef, pr, ctmp, ALU.mult).then_inc(s_cf, 1)
                if prev:
                    final(p, 1, (slot + 2) % 3)
                if main:
                    mask(i, 0)
                    mask(i, 1)
                if nxt:
                    conv_products(n, 0)
                    conv_products(n, 1)
                if nxt:
                    conv_sum(n)
                if main:
                    head_out(i, 0)
                    mask(i, 2)
                    head_out(i, 1)
                    mask(i, 3)
                if nxt2:
                    first_norm(i + 2, (slot + 2) % 3)
                if nxt:
                    h_low(n)
                if main:
                    head_out(i, 2)
                    head_out(i, 3)

            def final(p, g, slot):
                part = slice(g * HALF, (g + 1) * HALF)
                dve.wait_ge(s_up, 2 * p + g + 1)
                V.scalar_tensor_tensor(x_ring[:, slot, part], ps_g[g][:, :], usc[:, g:g + 1], x_ring[:, slot, part],
                                       ALU.mult, ALU.add).then_inc(s_fin, 1)

            def denominator_terms(n):
                dve.wait_ge(s_e, 2 * (n + 1))
                after(dve, s_hlo, 2 * n)
                after(dve, s_pre, n)
                recurrence_terms(n, ek[:, :], carry_b, s_sva, s_ekt, fa[:, :], s_fda)

            def denominator_scan(n):
                scan(n, s_fda, s_sca, carry_b, s_sva)
                add_state(fa[:, :], s_den)

            def numerator(n):
                dve.wait_ge(s_ev, n + 1)
                after(dve, s_yt, n)
                dve.wait_ge(s_den, n + 1)
                recurrence_terms(n, vx[:, :], carry_a, s_svb, s_evt, fb[:, :], s_fdb)
                scan(n, s_fdb, s_scb, carry_a, s_svb)
                add_state(fb[:, :], s_num)

            def recurrence_output(n, g):
                part = slice(g * HALF, (g + 1) * HALF)
                dve.wait_ge(s_den, n + 1)
                V.reciprocal(fa[:, part], fa[:, part]).then_inc(s_rec, 1)
                dve.wait_ge(s_num, n + 1)
                dve.wait_ge(s_rec, 2 * n + g + 1)
                V.tensor_tensor(fb[:, part], fb[:, part], fa[:, part], ALU.mult).then_inc(s_y, 1)

            def output_transpose(n):
                dve.wait_ge(s_y, 2 * (n + 1))
                V.transpose(fa[:, :], fb[:, :]).then_inc(s_yt, 1)

            def residual(n, slot):
                xs = x_ring[:, slot, :]
                dve.wait_ge(s_yt, n + 1)
                V.scalar_tensor_tensor(xs, fa[:, :], tg[:, 0:1], xs, ALU.mult, ALU.add).then_inc(s_x2, 1)
                dve.wait_ge(s_x2, n + 1)
                norm_stats(n, xs, st2, mv2, s_bn2, s_ag2)

            def conv_sum(n):
                dve.wait_ge(s_z, 2 * (n + 1))
                dve.wait_ge(s_z2, 2 * (n + 1))
                now = fa[:, :].rearrange("p (c n) -> p c n", n=P)[:, :, TT:P]
                past = seg[:, 0:C].rearrange("p (c n) -> p c n", n=P)[:, :, 0:P - TT]
                V.tensor_tensor(now, now, past, ALU.add).then_inc(s_pre, 1)

            def h_low(n):
                for g in range(2):
                    dve.wait_ge(s_hhi, 2 * n + g + 1)
                    part = slice(g * HALF, (g + 1) * HALF)
                    V.scalar_tensor_tensor(h_lo[:, part], fa[:, part], sw[:, U:U + 1], h_hi[:, part],
                                           ALU.mult, ALU.subtract).then_inc(s_hlo, 1)

            def conv_products(n, g):
                dve.wait_ge(s_x2, n + 1)
                dve.wait_ge(s_num, n + 1)
                dve.wait_ge(s_xnp, 2 * n + g + 1)
                V.tensor_tensor(fa[:, g * HALF:(g + 1) * HALF].rearrange("p (c n) -> p c n", n=P),
                                ps_t[g][:, :].rearrange("p (c n) -> p c n", n=P),
                                per_chunk(cw1, 4 * g, 4 * g + 4, P), ALU.mult).then_inc(s_z, 1)
                V.tensor_tensor(seg[:, g * HALF:(g + 1) * HALF].rearrange("p (c n) -> p c n", n=P),
                                ps_t[g][:, :].rearrange("p (c n) -> p c n", n=P),
                                per_chunk(cw0, 4 * g, 4 * g + 4, P), ALU.mult).then_inc(s_z2, 1)

            def mask(i, g):
                dve.wait_ge(s_sp, 4 * i + g + 1)
                after(dve, s_op, 4 * i + g - 1)
                if g < 2:
                    dve.wait_ge(s_ktp, i + 1)
                V.tensor_tensor(probs[g % 2].rearrange("p (h l) -> p h l", h=HG),
                                ps_s[g % 2][:, :].rearrange("p (h l) -> p h l", h=HG),
                                causal_m[:, :].rearrange("p (o l) -> p o l", o=1)
                                .to_broadcast([P, HG, P]), ALU.mult).then_inc(s_p, 1)

            def gate_scale(i):
                dve.wait_ge(s_sg, 2 * (i + 1))
                after(dve, s_us, i)
                V.tensor_reduce(gmx, sg, AX_X, ALU.max, apply_absolute_value=True).then_inc(s_gm, 1)
                dve.wait_ge(s_gm, i + 1)
                V.tensor_scalar(gmx, gmx, TINY, None, ALU.max).then_inc(s_gm2, 1)
                dve.wait_ge(s_gm2, i + 1)
                after(dve, s_gs, i)
                V.reciprocal(grc, gmx).then_inc(s_rg, 1)
                after(dve, s_fin, 2 * i)
                V.tensor_scalar(usc, base, gmx, HEAD_BOUND / G_TOP, ALU.mult, ALU.mult).then_inc(s_us, 1)
                dve.wait_ge(s_rg, i + 1)
                V.tensor_scalar(gsc, grc, G_TOP / HEAD_BOUND, None, ALU.mult).then_inc(s_gs, 1)

            def first_norm(j, slot):
                dve.wait_ge(s_x, 16 * (j + 1))
                norm_stats(j, x_ring[:, slot, :], st1, mv1, s_bn1, s_ag1)

            def head_out(i, g):
                dve.wait_ge(s_op, 4 * i + g + 1)
                after(dve, s_gtp, 2 * i)
                both = ps_o[g % 2][:, :].rearrange("p (h s d) -> p h s d", h=HG, s=2)
                part = by_head(tmp[:, g * HG * DV:(g + 1) * HG * DV], DV)
                V.tensor_tensor(part, both[:, :, 1, :], per_head(sgn, g * HG, (g + 1) * HG, DV), ALU.mult)\
                 .then_inc(s_ob, 1)
                dve.wait_ge(s_ob, 5 * i + g + 2)
                V.tensor_tensor(by_head(o_sb[:, g * HG * DV:(g + 1) * HG * DV], DV), both[:, :, 0, :], part,
                                ALU.add).then_inc(s_o, 1)

            for cols, value in ((nhalf, -0.5), (eps_c, EPS), (dv_c, 1.0 / DV), (shift1, -SHIFT), (shift2, 0.0)):
                V.memset(cols, value).then_inc(s_cv, 1)
            V.memset(carry_a[:, :], 0.0).then_inc(s_cv, 1)
            V.memset(carry_b[:, :], 0.0).then_inc(s_cv, 1)
            V.memset(decay[:, :], 0.0).then_inc(s_cv, 1)
            dve.wait_ge(s_const, 16 * 7)
            V.tensor_scalar(eu, eu, U_MAX, None, ALU.min).then_inc(s_cv, 1)
            first_norm(0, 0)
            dve.wait_ge(s_cv, 9)
            dve.wait_ge(s_ca, 6)
            V.tensor_copy(cbt(decay[:, :])[:, :, :, 1:SEG],
                          dk.rearrange("p (c o q) -> p c o q", o=1, q=1).to_broadcast([P, CB, BB, TT]))\
             .then_inc(s_cv, 1)
            V.tensor_tensor(delta[:, 0:KC], delta[:, 0:KC], sgn[:, 0:KC], ALU.add).then_inc(s_cv, 1)
            dve.wait_ge(s_cv, 11)
            V.tensor_reduce(mx[:, U:U + 1], delta[:, 0:KC], AX_X, ALU.max).then_inc(s_max, 1)
            scale_of(U, H_TOP / LN_BOUND, 1)
            denominator_terms(0)
            denominator_scan(0)
            set_scale(0)
            numerator(0)
            lo_unit(0)
            set_scale(1)
            recurrence_output(0, 0)
            set_scale(2)
            recurrence_output(0, 1)
            lo_unit(1)
            set_scale(3)
            output_transpose(0)
            residual(0, 0)
            set_scale(4)
            lo_unit(2)
            lo_unit(3)
            set_scale(5)
            conv_products(0, 0)
            conv_products(0, 1)
            conv_sum(0)
            dve.wait_ge(s_router, 16 * 7)
            V.tensor_tensor(router_d[:, :], router_d[:, :], x_ring[:, 2, :], ALU.subtract).then_inc(s_base, 1)
            first_norm(1, 1)
            h_low(0)
            lo_unit(4)
            set_scale(6)
            lo_unit(5)
            set_scale(7)
            lo_unit(6)
            for g in range(2):
                V.tensor_scalar(base[:, g:g + 1], mx[:, UO + g:UO + g + 1], tg[:, 1:2], 1.0 / W_TOP,
                                ALU.mult, ALU.mult).then_inc(s_base, 1)
            lo_unit(7)
            dve.wait_ge(s_base, 3)
            pipeline(dve, step)

        @block.gpsimd
        def _(pool):
            G = nc.gpsimd
            U = len(UNITS)

            def bound_all(u, s, count):
                pool.wait_ge(s, count)
                G.partition_all_reduce(mx[:, u:u + 1], mx[:, u:u + 1], P, AMAX).then_inc(s_wall, 1)

            def norm_scale(j, mv, ve, rs, nm, nb, shift, s_ag, s_rs, s_nb):
                pool.wait_ge(s_ag, j + 1)
                G.tensor_tensor(ve, mv[:, 1:2], eps_c[:, 0:1], ALU.add).then_inc(s_rs, 1)
                pool.wait_ge(s_rs, 3 * j + 1)
                G.tensor_tensor(rs, ve, nhalf[:, 0:1], ALU.pow).then_inc(s_rs, 1)
                pool.wait_ge(s_rs, 3 * j + 2)
                after(pool, s_nb, j)
                G.tensor_tensor(nm, mv[:, 0:1], rs, ALU.mult).then_inc(s_rs, 1)
                pool.wait_ge(s_rs, 3 * j + 3)
                G.tensor_tensor(nb, shift, nm, ALU.subtract).then_inc(s_nb, 1)

            def first_scale(j):
                norm_scale(j, mv1, ve1, rs1, nm1, nb1, shift1, s_ag1, s_rs1, s_nb1)

            def second_scale(j):
                norm_scale(j, mv2, ve2, rs2, nm2, nb2, shift2, s_ag2, s_rs2, s_nb2)

            def exp_kv(j):
                pool.wait_ge(s_e, 2 * (j + 1))
                pool.wait_ge(s_vl, 16 * (j + 1))
                G.tensor_tensor(vx[:, :], vx[:, :], ek[:, :], ALU.mult).then_inc(s_ev, 1)

            def head_factors(p):
                pool.wait_ge(s_ss, p + 1)
                pool.wait_ge(s_cf, p + 1)
                G.tensor_tensor(ftmp, coef, coef, ALU.mult).then_inc(s_fp, 1)
                pool.wait_ge(s_fp, 6 * p + 1)
                G.tensor_tensor(ftmp, ftmp, ossq, ALU.mult).then_inc(s_fp, 1)
                pool.wait_ge(s_fp, 6 * p + 2)
                G.tensor_tensor(ftmp, ftmp, dv_c, ALU.mult).then_inc(s_fp, 1)
                pool.wait_ge(s_fp, 6 * p + 3)
                G.tensor_tensor(ftmp, ftmp, eps_c, ALU.add).then_inc(s_fp, 1)
                pool.wait_ge(s_fp, 6 * p + 4)
                G.tensor_tensor(fac, ftmp, nhalf, ALU.pow).then_inc(s_fp, 1)
                pool.wait_ge(s_fp, 6 * p + 5)
                G.tensor_tensor(fac, fac, coef, ALU.mult).then_inc(s_fp, 1)
                pool.wait_ge(s_fp, 6 * p + 6)
                pool.wait_ge(s_gs, p + 1)
                G.tensor_tensor(fac, fac, gsc.to_broadcast([P, H]), ALU.mult).then_inc(s_f, 1)

            def step(i, slot, main, nxt, nxt2, prev):
                n, p = i + 1, i - 1
                if prev:
                    pool.wait_ge(s_sq, p + 1)
                    pool.wait_ge(s_sg, 2 * (p + 1))
                    G.tensor_tensor(o_sb, o_sb, sg, ALU.mult).then_inc(s_og, 1)
                    head_factors(p)
                if main:
                    pool.wait_ge(s_k, i + 1)
                    after(pool, s_op, 4 * i)
                    after(pool, s_o, 4 * i)
                    rotate(pool, G, i, 1, k_sb, rot_k, s_r1k, s_rk)
                    pool.wait_ge(s_rk, i + 1)
                    pool.wait_ge(s_rq, i + 1)
                    for g in range(2):
                        pool.wait_ge(s_vc, 2 * i + g + 1)
                        G.tensor_tensor(by_head(tmp[:, g * HALF:(g + 1) * HALF], DV), v2[:, g * 8:(g + 1) * 8, 0, :],
                                        by_head(router_d[:, g * HALF:(g + 1) * HALF], DV), ALU.mult)\
                         .then_inc(s_vr, 1)
                if nxt:
                    second_scale(n)
                if main:
                    pool.wait_ge(s_sgn, i + 1)
                    G.tensor_tensor(v2[:, :, 1, :], v2[:, :, 0, :], per_head(sgn, 0, H, DV), ALU.mult)\
                     .then_inc(s_sv, 1)
                if nxt2:
                    first_scale(i + 2)
                if nxt2:
                    exp_kv(i + 2)

            pool.wait_ge(s_cv, 8)
            first_scale(0)
            bound_all(U, s_max, 1)
            exp_kv(0)
            for u in range(5):
                bound_all(u, s_wsum, u + 1)
            second_scale(0)
            bound_all(5, s_wsum, 6)
            first_scale(1)
            for u in range(UO, U):
                n = u - UO
                pool.wait_ge(s_wpart, 2 * (n + 1))
                G.tensor_tensor(mx[:, u:u + 1], osum[:, 2 * n:2 * n + 1], osum[:, 2 * n + 1:2 * n + 2], ALU.add)\
                 .then_inc(s_wsum, 1)
                bound_all(u, s_wsum, u + 1)
            exp_kv(1)
            pool.wait_ge(s_router, 16 * 7)
            pool.wait_ge(s_base, 1)
            pipeline(pool, step)


_INPUTS = ("x", "ctx_2048", "g_xattn", "g_ffn", "decay", "first", "conv", "wq", "wk", "wv", "wg", "router", "wout",
           "identity", "causal", "cos", "sin", "count", "heads")


def _shape_constants():
    import numpy as np

    f = np.float32
    t, b = np.arange(P) % TT, np.arange(P) // TT
    inv_freq = (f(1.0) / f(10000.0) ** (np.arange(0, DK, 2, dtype=f) / f(DK))).astype(f)
    angle = b.astype(f)[:, None] * inv_freq[None, :]
    cos, sin = np.cos(angle).astype(f), np.sin(angle).astype(f)
    return {
        "identity": np.eye(P, dtype=f),
        "causal": ((t[:, None] == t[None, :]) & (b[:, None] <= b[None, :])).astype(f),
        "cos": np.concatenate([cos, cos], axis=1),
        "sin": np.concatenate([-sin, sin], axis=1),
        "count": (b + 1).astype(f)[:, None],
        "heads": (np.arange(P)[:, None] // DK == np.arange(HG)[None, :]).astype(f),
    }


def kernel(**inputs):
    import numpy as np
    import concourse.bacc as bacc
    from concourse.bass_utils import run_bass_kernel_spmd

    a = {n: np.asarray(v) for n, v in inputs.items()}
    layout = {
        "x": a["x"], "ctx_2048": a["ctx_2048"],
        "g_xattn": a["g_xattn"].reshape(1, 1), "g_ffn": a["g_ffn"].reshape(1, 1),
        "decay": np.tile(a["L0_xattn_time_decay"].reshape(CB, SQ).T, (P // SQ, 1)),
        "first": np.tile(a["L0_xattn_time_first"].reshape(CB, SQ).T, (P // SQ, 1)),
        "conv": a["L0_ffn_conv_w"].reshape(KC, P, 2).transpose(2, 1, 0),
        "wq": a["L0_ffn_Wq"], "wk": a["L0_ffn_Wk"], "wv": a["L0_ffn_Wv"], "wg": a["L0_ffn_Wg"],
        "router": a["L0_ffn_router_w"].reshape(C, 2).T, "wout": a["L0_ffn_Wout"],
        **_shape_constants(),
    }
    nc = bacc.Bacc("TRN2", target_bir_lowering=False, num_devices=1)
    arrays, args = {}, []
    for name in _INPUTS:
        arr = np.ascontiguousarray(layout[name])
        arrays[f"in_{name}"] = arr
        args.append(nc.dram_tensor(f"in_{name}", arr.shape, mybir.dt.from_np(arr.dtype), kind="ExternalInput").ap())
    out = nc.dram_tensor("out", a["x"].shape, F32, kind="ExternalOutput").ap()
    flamingo_layer(nc, *args, out)
    r = run_bass_kernel_spmd(nc, [arrays], core_ids=[0])
    return r.results[0]["out"]
```
